# Optimizing a Trainium2 kernel written in Bass

```python
import numpy as np
import jax
import jax.numpy as jnp

def _softmax(x, axis=-1):
    return jax.nn.softmax(x, axis=axis)

def _gelu(x):
    return jax.nn.gelu(x, approximate=True)

def _silu(x):
    return jax.nn.silu(x)

def _sigmoid(x):
    return jax.nn.sigmoid(x)

def _layernorm(x, axis=-1, eps=1e-05):
    m = jnp.mean(x, axis=axis, keepdims=True)
    v = jnp.var(x, axis=axis, keepdims=True)
    return (x - m) / jnp.sqrt(v + eps)

def _scatter_add(tgt, idx, src, axis=0):
    return tgt.at[idx].add(src)

def _segment_sum(src, seg, n):
    return jax.ops.segment_sum(src, seg, n)
kernel_name = 'mk_dlrm_tower_d1_rec_r8_6eff44'

def setup_inputs(seed: int=0):
    np.random.seed(seed)
    _w = jnp.asarray

    def _rec_inputs():
        import jax
        import jax.numpy as jnp
        _tk = jax.random.key(seed)
        ids = jnp.stack([jax.random.randint(jax.random.fold_in(_tk, 200 + f), (2048,), 0, v, jnp.int32) for f, v in enumerate([1000, 1000, 12500, 1000, 1000, 1250, 1000, 125000, 12500, 1000, 1000, 12500, 12500, 1000, 1250, 1000, 1000, 12500, 1250, 1000, 1250, 1000, 1250, 1000, 1000, 1250])], axis=1)
        tbl_0 = 0.05 * jax.random.normal(jax.random.fold_in(_tk, 500 + 0), (1000, 128), jnp.float32)
        tbl_1 = 0.05 * jax.random.normal(jax.random.fold_in(_tk, 500 + 1), (1000, 128), jnp.float32)
        tbl_2 = 0.05 * jax.random.normal(jax.random.fold_in(_tk, 500 + 2), (12500, 128), jnp.float32)
        tbl_3 = 0.05 * jax.random.normal(jax.random.fold_in(_tk, 500 + 3), (1000, 128), jnp.float32)
        tbl_4 = 0.05 * jax.random.normal(jax.random.fold_in(_tk, 500 + 4), (1000, 128), jnp.float32)
        tbl_5 = 0.05 * jax.random.normal(jax.random.fold_in(_tk, 500 + 5), (1250, 128), jnp.float32)
        tbl_6 = 0.05 * jax.random.normal(jax.random.fold_in(_tk, 500 + 6), (1000, 128), jnp.float32)
        tbl_7 = 0.05 * jax.random.normal(jax.random.fold_in(_tk, 500 + 7), (125000, 128), jnp.float32)
        tbl_8 = 0.05 * jax.random.normal(jax.random.fold_in(_tk, 500 + 8), (12500, 128), jnp.float32)
        tbl_9 = 0.05 * jax.random.normal(jax.random.fold_in(_tk, 500 + 9), (1000, 128), jnp.float32)
        tbl_10 = 0.05 * jax.random.normal(jax.random.fold_in(_tk, 500 + 10), (1000, 128), jnp.float32)
        tbl_11 = 0.05 * jax.random.normal(jax.random.fold_in(_tk, 500 + 11), (12500, 128), jnp.float32)
        tbl_12 = 0.05 * jax.random.normal(jax.random.fold_in(_tk, 500 + 12), (12500, 128), jnp.float32)
        tbl_13 = 0.05 * jax.random.normal(jax.random.fold_in(_tk, 500 + 13), (1000, 128), jnp.float32)
        tbl_14 = 0.05 * jax.random.normal(jax.random.fold_in(_tk, 500 + 14), (1250, 128), jnp.float32)
        tbl_15 = 0.05 * jax.random.normal(jax.random.fold_in(_tk, 500 + 15), (1000, 128), jnp.float32)
        tbl_16 = 0.05 * jax.random.normal(jax.random.fold_in(_tk, 500 + 16), (1000, 128), jnp.float32)
        tbl_17 = 0.05 * jax.random.normal(jax.random.fold_in(_tk, 500 + 17), (12500, 128), jnp.float32)
        tbl_18 = 0.05 * jax.random.normal(jax.random.fold_in(_tk, 500 + 18), (1250, 128), jnp.float32)
        tbl_19 = 0.05 * jax.random.normal(jax.random.fold_in(_tk, 500 + 19), (1000, 128), jnp.float32)
        tbl_20 = 0.05 * jax.random.normal(jax.random.fold_in(_tk, 500 + 20), (1250, 128), jnp.float32)
        tbl_21 = 0.05 * jax.random.normal(jax.random.fold_in(_tk, 500 + 21), (1000, 128), jnp.float32)
        tbl_22 = 0.05 * jax.random.normal(jax.random.fold_in(_tk, 500 + 22), (1250, 128), jnp.float32)
        tbl_23 = 0.05 * jax.random.normal(jax.random.fold_in(_tk, 500 + 23), (1000, 128), jnp.float32)
        tbl_24 = 0.05 * jax.random.normal(jax.random.fold_in(_tk, 500 + 24), (1000, 128), jnp.float32)
        tbl_25 = 0.05 * jax.random.normal(jax.random.fold_in(_tk, 500 + 25), (1250, 128), jnp.float32)
        _rk = jax.random.fold_in(_tk, 7)
        r_dense_output = -0.000520686 + 1.00062 * jax.random.normal(jax.random.fold_in(_rk, 101), (2048, 128), jnp.float32)
        W_top1 = 0.0405887 * jax.random.normal(jax.random.fold_in(_tk, 801), (607, 512), jnp.float32)
        W_top2 = 0.0441942 * jax.random.normal(jax.random.fold_in(_tk, 802), (512, 256), jnp.float32)
        W_top3 = 0.0625 * jax.random.normal(jax.random.fold_in(_tk, 803), (256, 1), jnp.float32)
        b_top1 = jnp.zeros((512,), jnp.float32)
        b_top2 = jnp.zeros((256,), jnp.float32)
        return (r_dense_output, ids, tbl_0, tbl_1, tbl_2, tbl_3, tbl_4, tbl_5, tbl_6, tbl_7, tbl_8, tbl_9, tbl_10, tbl_11, tbl_12, tbl_13, tbl_14, tbl_15, tbl_16, tbl_17, tbl_18, tbl_19, tbl_20, tbl_21, tbl_22, tbl_23, tbl_24, tbl_25, W_top1, b_top1, W_top2, b_top2, W_top3)
    r_dense_output, ids, tbl_0, tbl_1, tbl_2, tbl_3, tbl_4, tbl_5, tbl_6, tbl_7, tbl_8, tbl_9, tbl_10, tbl_11, tbl_12, tbl_13, tbl_14, tbl_15, tbl_16, tbl_17, tbl_18, tbl_19, tbl_20, tbl_21, tbl_22, tbl_23, tbl_24, tbl_25, W_top1, b_top1, W_top2, b_top2, W_top3 = _rec_inputs()

    def _L0_rec_setup():
        import jax, jax.numpy as jnp
        import numpy as np
        B, NUM_SPARSE, D = (2048, 26, 128)
        key = jax.random.key(seed)
        k1, k2 = jax.random.split(key)
        dense_output = jax.random.normal(k1, (B, D), dtype=jnp.float32)
        embeddings = jax.random.normal(k2, (B, NUM_SPARSE, D), dtype=jnp.float32)
        return {'dense_output': dense_output, 'embeddings': embeddings}
    _L0_rec_all = _L0_rec_setup()
    _L0_rec_in = {k: v for k, v in _L0_rec_all.items() if k in ()}
    del _L0_rec_all
    return {'r_dense_output': r_dense_output, 'ids': ids, 'tbl_0': tbl_0, 'tbl_1': tbl_1, 'tbl_2': tbl_2, 'tbl_3': tbl_3, 'tbl_4': tbl_4, 'tbl_5': tbl_5, 'tbl_6': tbl_6, 'tbl_7': tbl_7, 'tbl_8': tbl_8, 'tbl_9': tbl_9, 'tbl_10': tbl_10, 'tbl_11': tbl_11, 'tbl_12': tbl_12, 'tbl_13': tbl_13, 'tbl_14': tbl_14, 'tbl_15': tbl_15, 'tbl_16': tbl_16, 'tbl_17': tbl_17, 'tbl_18': tbl_18, 'tbl_19': tbl_19, 'tbl_20': tbl_20, 'tbl_21': tbl_21, 'tbl_22': tbl_22, 'tbl_23': tbl_23, 'tbl_24': tbl_24, 'tbl_25': tbl_25, 'W_top1': W_top1, 'b_top1': b_top1, 'W_top2': W_top2, 'b_top2': b_top2, 'W_top3': W_top3}

def reference(r_dense_output, ids, tbl_0, tbl_1, tbl_2, tbl_3, tbl_4, tbl_5, tbl_6, tbl_7, tbl_8, tbl_9, tbl_10, tbl_11, tbl_12, tbl_13, tbl_14, tbl_15, tbl_16, tbl_17, tbl_18, tbl_19, tbl_20, tbl_21, tbl_22, tbl_23, tbl_24, tbl_25, W_top1, b_top1, W_top2, b_top2, W_top3):
    import jax
    import jax.numpy as jnp

    def _L0_rec_ref(dense_output, embeddings):
        import jax, jax.numpy as jnp
        import numpy as np
        B, NUM_SPARSE, D = (2048, 26, 128)
        combined = jnp.concatenate([dense_output[:, None, :], embeddings], axis=1)
        interactions = jnp.einsum('bfd,bgd->bfg', combined, combined)
        F = combined.shape[1]
        iu, ju = jnp.triu_indices(F, k=1)
        interactions_flat = interactions[:, iu, ju]
        return jnp.concatenate([dense_output, interactions_flat], axis=1)
    e = jnp.stack([tbl_0[ids[:, 0]], tbl_1[ids[:, 1]], tbl_2[ids[:, 2]], tbl_3[ids[:, 3]], tbl_4[ids[:, 4]], tbl_5[ids[:, 5]], tbl_6[ids[:, 6]], tbl_7[ids[:, 7]], tbl_8[ids[:, 8]], tbl_9[ids[:, 9]], tbl_10[ids[:, 10]], tbl_11[ids[:, 11]], tbl_12[ids[:, 12]], tbl_13[ids[:, 13]], tbl_14[ids[:, 14]], tbl_15[ids[:, 15]], tbl_16[ids[:, 16]], tbl_17[ids[:, 17]], tbl_18[ids[:, 18]], tbl_19[ids[:, 19]], tbl_20[ids[:, 20]], tbl_21[ids[:, 21]], tbl_22[ids[:, 22]], tbl_23[ids[:, 23]], tbl_24[ids[:, 24]], tbl_25[ids[:, 25]]], axis=1)
    z = _L0_rec_ref(r_dense_output, e)
    z = z.reshape(z.shape[0], -1)
    h = jnp.concatenate([z, r_dense_output], axis=1)
    h = jnp.maximum(h @ W_top1 + b_top1, 0.0)
    h = jnp.maximum(h @ W_top2 + b_top2, 0.0)
    y = h @ W_top3
    return y

_drawn_inputs = setup_inputs


def setup_inputs(seed=0):
    import zlib

    import numpy as np

    out = dict(_drawn_inputs(seed))
    spreads = {'b_top1': (0.0, 0.1), 'b_top2': (0.0, 0.1)}
    factors = {}
    for name, (base, spread) in spreads.items():
        noise = np.random.default_rng([zlib.crc32(name.encode()), seed]).standard_normal(out[name].shape)
        drawn = base * np.exp(spread * noise) if base else spread * noise
        out[name] = jnp.asarray(drawn.astype(out[name].dtype))
    for name, factor in factors.items():
        out[name] = (out[name] * factor).astype(out[name].dtype)
    return out
```

```python
import concourse.bass as bass
from concourse import mybir
from contextlib import ExitStack

P = 128
QUAD = 32
B, D = 2048, 128
SPARSE = 26
F = SPARSE + 1
PAIRS = F * (F - 1) // 2
G = F - 1
N1, N2 = 512, 256
TILES = 2
CHUNK = TILES * P
CHUNKS = B // CHUNK
TG = 4
TGROUPS = -(-F // TG)
SQ = P // QUAD
MB = 4
BANKS = 2
PG_SAMPLES = BANKS * MB * SQ
PGROUPS = P // PG_SAMPLES
KI = -(-G // 4)
NB1, NB2 = N1 // P, N2 // P


def k_rows(i):
    return QUAD * min(4, G - 4 * i)


def pair_row(p, g):
    return D + p * F - p * (p + 1) // 2 + (g - p - 1)


def dlrm_tower(nc, dense, ids, tables, w_top1, b_top1, w_top2, b_top2, w_top3, out):
    fp32 = mybir.dt.float32
    i32 = mybir.dt.int32
    ALU = mybir.AluOpType
    ACT = mybir.ActivationFunctionType

    with ExitStack() as ctx:
        def sbuf(name, shape, dt=fp32):
            return ctx.enter_context(nc.sbuf_tensor(name, shape, dt))

        def psum(name, shape):
            return ctx.enter_context(nc.psum_tensor(name, shape, fp32))

        def sem(name):
            return ctx.enter_context(nc.semaphore(name))

        idx = [sbuf(f"idx{h}", [P, SPARSE], i32) for h in range(TILES)]
        X = [sbuf(f"X{h}", [P, F, D]) for h in range(TILES)]
        XT = [sbuf(f"XT{h}", [D, P, QUAD]) for h in range(TILES)]
        XD = sbuf("XD", [D, CHUNK])
        I = sbuf("I", [P, KI, CHUNK])
        W1 = sbuf("W1", [P, KI, N1])
        W1D = sbuf("W1D", [D, 2, N1])
        W2 = sbuf("W2", [P, NB1, N2])
        W3 = sbuf("W3", [P, NB2])
        b1 = sbuf("b1", [P, NB1])
        b2 = sbuf("b2", [P, NB2])
        h1 = sbuf("h1", [P, NB1, CHUNK])
        h2 = sbuf("h2", [P, NB2, CHUNK])
        y = sbuf("y", [1, B])
        ident = sbuf("ident", [P, P])

        Tps = psum("Tps", [P, 2, TG, P])
        Gps = psum("Gps", [P, 2, BANKS, 512])
        Hps = psum("Hps", [P, 2, 512])[:, :, 0:CHUNK]

        ids_landed = [sem(f"ids_landed{h}") for h in range(TILES)]
        dense_landed = [sem(f"dense_landed{h}") for h in range(TILES)]
        x_landed = [[sem(f"x_landed{h}_{t}") for t in range(TGROUPS)] for h in range(TILES)]
        gathers_begun = sem("gathers_begun")
        w1_landed = sem("w1_landed")
        w1d_landed = sem("w1d_landed")
        mlp_landed = sem("mlp_landed")
        w1_zeroed = sem("w1_zeroed")
        pads_zeroed = sem("pads_zeroed")
        ident_zeroed = sem("ident_zeroed")
        ident_ready = sem("ident_ready")
        w1d_summed = sem("w1d_summed")
        transposed = sem("transposed")
        xt_ready = sem("xt_ready")
        xd_ready = sem("xd_ready")
        products_done = sem("products_done")
        pairs_ready = sem("pairs_ready")
        l1_done = sem("l1_done")
        h1_ready = sem("h1_ready")
        l2_done = sem("l2_done")
        h2_ready = sem("h2_ready")
        l3_done = sem("l3_done")
        y_ready = sem("y_ready")
        y_stored = sem("y_stored")

        def t_count(c, h, t):
            return (c * TILES + h) * TGROUPS + t + 1

        def p_count(c, h, k):
            return (c * TILES + h) * PGROUPS + k + 1

        def tg_features(t):
            return range(t * TG, min(F, t * TG + TG))

        W1_LOADS = [(p, j) for p in range(F - 1) for j in range(4)
                    if any(1 + j + 4 * i > p and 1 + j + 4 * i < F for i in range(KI))]

        def load_w1(eng, p, j):
            i0 = next(i for i in range(KI) if 1 + j + 4 * i > p)
            n = len(range(1 + j + 4 * i0, F, 4))
            row = pair_row(p, 1 + j + 4 * i0)
            at = QUAD * j + p
            eng.dma_start(W1[at:at + 1, i0:i0 + n, :],
                          w_top1[row:row + 4 * (n - 1) + 1:4, :].rearrange("(o i) n -> o i n", o=1)
                          ).then_inc(w1_landed, 16)

        block = ctx.enter_context(nc.Block())

        @block.sync
        def _(sp):
            def load_tile(c, h, first):
                rows = bass.ds(c * CHUNK + h * P if first else sp.snap(c * CHUNK + h * P), P)
                if not first:
                    sp.wait_ge(transposed, t_count(c - 1, h, TGROUPS - 1))
                sp.dma_start(idx[h][:, :], ids[rows, :]).then_inc(ids_landed[h], 16)
                sp.dma_start(X[h][:, 0, :], dense[rows, :]).then_inc(dense_landed[h], 16)

            load_tile(0, 0, True)
            load_tile(0, 1, True)
            sp.wait_ge(w1_zeroed, 1)
            for p, j in W1_LOADS[0::2]:
                load_w1(sp, p, j)
            with sp.Fori(1, CHUNKS) as c:
                load_tile(c, 0, False)
                load_tile(c, 1, False)
            sp.wait_ge(y_ready, CHUNKS)
            sp.dma_start(out.rearrange("b o -> o b"), y[:, :]).then_inc(y_stored, 16)
            sp.wait_ge(y_stored, 16)

        @block.gpsimd
        def _(pool):
            pool.memset(ident[:, :], 0.0).then_inc(ident_zeroed, 1)
            pool.wait_ge(ident_zeroed, 1)
            pool.affine_select(out=ident[:, :], in_=ident[:, :], compare_op=ALU.not_equal, fill=1.0,
                               base=0, pattern=[[-1, P]], channel_multiplier=1).then_inc(ident_ready, 1)

            def gather_tile(c, h):
                pool.wait_ge(ids_landed[h], (c + 1) * 16)
                pool.sem_inc(gathers_begun, 1)
                for t in range(TGROUPS):
                    for f in tg_features(t):
                        if f:
                            pool.indirect_dma_start(
                                X[h][:, f, :], None, tables[f - 1][:, :],
                                bass.IndirectOffsetOnAxis(idx[h][:, f - 1:f], 0)).then_inc(x_landed[h][t], 16)

            gather_tile(0, 0)
            gather_tile(0, 1)
            with pool.Fori(1, CHUNKS) as c:
                gather_tile(c, 0)
                gather_tile(c, 1)

        @block.scalar
        def _(act):
            for k in range(2):
                act.dma_start(W1D[:, k, :], w_top1[k * (D + PAIRS):k * (D + PAIRS) + D, :]).then_inc(w1d_landed, 16)
            act.wait_ge(w1_zeroed, 1)
            for p, j in W1_LOADS[1::2]:
                load_w1(act, p, j)
            act.dma_start(W2[:, :, :], w_top2.rearrange("(k p) n -> p k n", p=P)).then_inc(mlp_landed, 16)
            with nc.allow_non_contiguous_dma(reason="1280 values in all, once"):
                act.dma_start(b1[:, :], b_top1.rearrange("(k p) -> p k", p=P)).then_inc(mlp_landed, 16)
                act.dma_start(b2[:, :], b_top2.rearrange("(k p) -> p k", p=P)).then_inc(mlp_landed, 16)
                act.dma_start(W3[:, :], w_top3.rearrange("(k p) o -> p (k o)", p=P)).then_inc(mlp_landed, 16)

            def features_out(c, h, first):
                if not first:
                    act.wait_ge(products_done, p_count(c - 1, h, PGROUPS - 1))
                    act.wait_ge(xd_ready, (c - 1) * TILES + h + 1)
                for t in range(TGROUPS):
                    n = len(tg_features(t))
                    act.wait_ge(transposed, t_count(c, h, t))
                    act.activation(XT[h][:, :, t * TG:t * TG + n],
                                   Tps[:, (h * TGROUPS + t) % 2, 0:n, :].rearrange("d f b -> d b f"),
                                   ACT.Copy).then_inc(xt_ready, 1)

            def mlp_out(c):
                for n in range(NB1):
                    act.wait_ge(l1_done, c * NB1 + n + 1)
                    act.activation(h1[:, n, :], Hps[:, n % 2, :], ACT.Relu,
                                   bias=b1[:, n:n + 1]).then_inc(h1_ready, 1)
                for m in range(NB2):
                    act.wait_ge(l2_done, c * NB2 + m + 1)
                    act.activation(h2[:, m, :], Hps[:, m, :], ACT.Relu,
                                   bias=b2[:, m:m + 1]).then_inc(h2_ready, 1)
                act.wait_ge(l3_done, c + 1)
                act.activation(y[0:1, bass.ds(c * CHUNK, CHUNK)], Hps[0:1, 0, :], ACT.Copy).then_inc(y_ready, 1)

            features_out(0, 0, True)
            features_out(0, 1, True)
            act.wait_ge(mlp_landed, 4 * 16)
            with act.Fori(1, CHUNKS) as c:
                features_out(c, 0, False)
                features_out(c, 1, False)
                mlp_out(c - 1)
            mlp_out(CHUNKS - 1)

        @block.vector
        def _(dve):
            dve.memset(W1[:, :, :], 0.0).then_inc(w1_zeroed, 1)
            for h in range(TILES):
                dve.memset(XT[h][:, :, F:QUAD], 0.0).then_inc(pads_zeroed, 1)
            dve.wait_ge(w1d_landed, 2 * 16)
            dve.tensor_tensor(W1D[:, 0, :], W1D[:, 0, :], W1D[:, 1, :], ALU.add).then_inc(w1d_summed, 1)

            def pairs_out(c, h, first):
                if h == 0 and not first:
                    dve.wait_ge(l1_done, c * NB1)
                dve.wait_ge(xt_ready, t_count(c, h, 0))
                dve.tensor_copy(XD[:, h * P:(h + 1) * P], XT[h][:, :, 0]).then_inc(xd_ready, 1)
                for k in range(PGROUPS):
                    dve.wait_ge(products_done, p_count(c, h, k))
                    b0 = h * P + k * PG_SAMPLES
                    for q in range(SQ):
                        src = Gps[QUAD * q:QUAD * (q + 1), k % 2, :, 0:MB * SQ * G].rearrange(
                            "p a (m s g) -> p a m s g", m=MB, s=SQ)
                        for j in range(4):
                            n = len(range(j, G, 4))
                            dst = I[QUAD * j:QUAD * (j + 1), 0:n, b0:b0 + PG_SAMPLES].rearrange(
                                "p i (a m s) -> p a m s i", a=BANKS, m=MB)
                            last = dve.tensor_copy(dst[:, :, :, q, :], src[:, :, :, q, j:G:4])
                    last.then_inc(pairs_ready, 1)

            pairs_out(0, 0, True)
            with dve.Fori(1, CHUNKS) as c:
                pairs_out(c - 1, 1, False)
                pairs_out(c, 0, False)
            pairs_out(CHUNKS - 1, 1, False)

        @block.tensor
        def _(pe):
            def transpose_tile(c, h, first):
                pe.wait_ge(dense_landed[h], 16 * (c + 1))
                for t in range(TGROUPS):
                    pe.wait_ge(x_landed[h][t], 16 * sum(f > 0 for f in tg_features(t)) * (c + 1))
                    if not (first and h == 0 and t < 2):
                        pe.wait_ge(xt_ready, t_count(c, h, t) - 2)
                    for s, f in enumerate(tg_features(t)):
                        last = pe.transpose(Tps[:, (h * TGROUPS + t) % 2, s, :], X[h][:, f, :], ident[:, :])
                    last.then_inc(transposed, 1)

            def products(c, h, first):
                pe.wait_ge(xt_ready, t_count(c, h, TGROUPS - 1))
                for k in range(PGROUPS):
                    if not (first and k < 2):
                        pe.wait_ge(pairs_ready, p_count(c, h, k) - 2)
                    for m in range(BANKS * MB):
                        b = k * PG_SAMPLES + m * SQ
                        last = pe.matmul(Gps[:, k % 2, m // MB, (m % MB) * SQ * G:(m % MB + 1) * SQ * G],
                                         XT[h][:, b:b + SQ, :], XT[h][:, b:b + SQ, 1:F], start=True, stop=True)
                    last.then_inc(products_done, 1)

            def mlp(c, first):
                pe.wait_ge(pairs_ready, p_count(c, 1, PGROUPS - 1))
                pe.wait_ge(xd_ready, (c + 1) * TILES)
                for n in range(NB1):
                    if n == 0 and not first:
                        pe.wait_ge(y_ready, c)
                    if n >= 2:
                        pe.wait_ge(h1_ready, c * NB1 + n - 1)
                    cols = slice(n * P, (n + 1) * P)
                    for i in range(KI):
                        pe.matmul(Hps[:, n % 2, :], W1[0:k_rows(i), i, cols], I[0:k_rows(i), i, :],
                                  start=(i == 0), stop=False)
                    pe.matmul(Hps[:, n % 2, :], W1D[:, 0, cols], XD[:, :],
                              start=False, stop=True).then_inc(l1_done, 1)
                pe.wait_ge(h1_ready, (c + 1) * NB1)
                for m in range(NB2):
                    for k in range(NB1):
                        last = pe.matmul(Hps[:, m, :], W2[:, k, m * P:(m + 1) * P], h1[:, k, :],
                                         start=(k == 0), stop=(k == NB1 - 1))
                    last.then_inc(l2_done, 1)
                pe.wait_ge(h2_ready, (c + 1) * NB2)
                for m in range(NB2):
                    last = pe.matmul(Hps[0:1, 0, :], W3[:, m:m + 1], h2[:, m, :],
                                     start=(m == 0), stop=(m == NB2 - 1))
                last.then_inc(l3_done, 1)

            pe.wait_ge(ident_ready, 1)
            transpose_tile(0, 0, True)
            transpose_tile(0, 1, False)
            pe.wait_ge(pads_zeroed, 2)
            products(0, 0, True)
            pe.wait_ge(w1_landed, 16 * len(W1_LOADS))
            pe.wait_ge(w1d_summed, 1)
            pe.wait_ge(mlp_landed, 4 * 16)
            transpose_tile(1, 0, False)
            products(0, 1, False)
            transpose_tile(1, 1, False)
            mlp(0, True)
            products(1, 0, False)
            with pe.Fori(2, CHUNKS) as c:
                transpose_tile(c, 0, False)
                products(c - 1, 1, False)
                transpose_tile(c, 1, False)
                mlp(c - 1, False)
                products(c, 0, False)
            products(CHUNKS - 1, 1, False)
            mlp(CHUNKS - 1, False)


_INS = (['r_dense_output', 'ids'] + [f'tbl_{i}' for i in range(SPARSE)]
        + ['W_top1', 'b_top1', 'W_top2', 'b_top2', 'W_top3'])


def kernel(**inputs):
    import numpy as _np
    import concourse.bacc as _bacc
    from concourse import mybir as _mybir
    from concourse.bass_utils import run_bass_kernel_spmd as _run

    nc = _bacc.Bacc("TRN2", target_bir_lowering=False, num_devices=1)
    arrays, args = {}, []
    for name in _INS:
        a = _np.ascontiguousarray(inputs[name])
        arrays[f"in_{name}_dram"] = a
        args.append(nc.dram_tensor(f"in_{name}_dram", a.shape, _mybir.dt.from_np(a.dtype), kind="ExternalInput").ap())
    out = nc.dram_tensor("out_0_dram", (B, 1), _mybir.dt.float32, kind="ExternalOutput").ap()
    dlrm_tower(nc, args[0], args[1], args[2:2 + SPARSE], *args[2 + SPARSE:], out)
    r = _run(nc, [arrays], core_ids=[0])
    return r.results[0]["out_0_dram"]
```

```python
import concourse.bass as bass
from concourse import mybir
from contextlib import ExitStack

P = 128
QUAD = 32
B, D = 2048, 128
SPARSE = 26
F = SPARSE + 1
PAIRS = F * (F - 1) // 2
G = F - 1
N1, N2 = 512, 256
TILES = 2
CHUNK = TILES * P
CHUNKS = B // CHUNK
BANK = 512

LOOKUPS = [1, 2, 4, 5, 7, 10, 20]
VOCAB, VK = 1000, 8
VP = VOCAB // VK
U = len(LOOKUPS)
PARTS = 2
PRODUCTS_OF_PARTS = [(0, 0), (1, 0), (0, 1)]
ONEHOTS = 3
SG = BANK // CHUNK
SGROUPS = [list(range(u, min(U, u + SG))) for u in range(0, U, SG)]
NS = len(SGROUPS)
ID_RUNS = []
for u in range(U):
    if u and LOOKUPS[u] == LOOKUPS[u - 1] + 1:
        ID_RUNS[-1][1] += 1
    else:
        ID_RUNS.append([u, 1])
LATER_TILES = B // P - TILES
TURNED = BANK // P
TURNS = [range(t, min(LATER_TILES, t + TURNED)) for t in range(0, LATER_TILES, TURNED)]

TGROUPS = [[0, 3, 6, 9], [8, 11, 14, 17], [12, 15, 18, 21], [13, 16, 19, 22], [23, 24, 25, 26]]
NT = len(TGROUPS)
XSLOTS = [s for slots in TGROUPS for s in slots]
assert sorted(XSLOTS + LOOKUPS) == list(range(F)) and XSLOTS[0] == 0

FEATURES = [("lookup", 0), ("lookup", 1)]
for n in range(max(NT, U - 2)):
    FEATURES += [(0, n)] * (n < NT) + [("lookup", n + 2)] * (n + 2 < U)
FILL_ORDER = FEATURES + [(1, t) for t in range(NT)]
FILL_BANK = [i % 4 for i in range(len(FEATURES))] + [t % 2 for t in range(NT)]
MLP_BANK = 2

SQ = P // QUAD
MB = 4
BANKS = 2
PG_SAMPLES = BANKS * MB * SQ
PGROUPS = P // PG_SAMPLES
DVE_QUADRANTS, ACT_QUADRANTS = (0, 1, 2), (3,)
MIXED = [("transpose", 0), ("transpose", 1)]
for n in range(max(NT - 2, PGROUPS)):
    MIXED += [("products", n)] * (n < PGROUPS) + [("transpose", n + 2)] * (n + 2 < NT)
KP = -(-PAIRS // P)
NB1, NB2 = N1 // P, N2 // P


def k_rows(i):
    return min(P, PAIRS - i * P)


def packs():
    row = 0
    for p in range(F - 1):
        g = p + 1
        while g < F:
            n = min(F - g, P - row % P)
            yield p, g, n, row
            g, row = g + n, row + n


PACKS = list(packs())
PAIR_BLOCKS = [(slice(0, P), slice(0, KP - 1)), (slice(0, k_rows(KP - 1)), slice(KP - 1, KP))]
POOL_PIECES = [[piece for n, piece in enumerate(PACKS) if piece[3] // P == i and n % 5 in (1, 3)] for i in range(KP)]
SP_PIECES = [[piece for n, piece in enumerate(PACKS) if piece[3] // P == i and n % 5 not in (1, 3)] for i in range(KP)]


def step_slice(slots):
    step = slots[1] - slots[0] if len(slots) > 1 else 1
    return slice(slots[0], slots[-1] + 1, step)


def former_use(order, i, c):
    same = [n for n in range(len(order)) if order[n] == order[i]]
    before = [n for n in same if n < i]
    return (before[-1], c) if before else (same[-1], c - 1)


def dlrm_tower(nc, dense, ids, tables, w_top1, b_top1, w_top2, b_top2, w_top3, out):
    fp32 = mybir.dt.float32
    fp32r = mybir.dt.float32r
    fp16 = mybir.dt.float16
    i32 = mybir.dt.int32
    ALU = mybir.AluOpType
    ACT = mybir.ActivationFunctionType

    with ExitStack() as ctx:
        def sbuf(name, shape, dt=fp32):
            return ctx.enter_context(nc.sbuf_tensor(name, shape, dt))

        def psum(name, shape):
            return ctx.enter_context(nc.psum_tensor(name, shape, fp32))

        def sem(name):
            return ctx.enter_context(nc.semaphore(name))

        idx = [sbuf(f"idx{h}", [P, SPARSE], i32) for h in range(TILES)]
        lidx16 = sbuf("lidx16", [P, TILES, SPARSE], fp16)
        later_ids = sbuf("later_ids", [P, LATER_TILES, SPARSE], i32)
        later_ids16 = sbuf("later_ids16", [P, LATER_TILES, U], fp16)
        turned_ids = nc.dram_tensor("turned_ids", (U, B - CHUNK), fp16, kind="Internal").ap()
        lidx_all = sbuf("lidx_all", [P, U, CHUNK], fp16)
        X = [sbuf(f"X{h}", [P, len(XSLOTS), D]) for h in range(TILES)]
        XT = sbuf("XT", [D, TILES, P, QUAD])
        XD = sbuf("XD", [D, PARTS, CHUNK], fp32r)
        scratch = sbuf("scratch", [P, G * CHUNK])
        I = scratch[0:QUAD, :].rearrange("p (g b) -> p g b", g=G)
        STAGES = G * CHUNK // (VK * D)
        tbl32 = [scratch[0:VP, i * VK * D:(i + 1) * VK * D].rearrange("p (k d) -> p k d", k=VK)
                 for i in range(STAGES)]
        XP = sbuf("XP", [P, KP, CHUNK])
        XPR = sbuf("XPR", [P, PARTS, KP, CHUNK], fp32r)
        W1 = sbuf("W1", [P, PARTS, KP, N1], fp32r)
        W1D = sbuf("W1D", [D, PARTS, N1], fp32r)
        W2 = sbuf("W2", [P, NB1, N2])
        W3 = sbuf("W3", [P, NB2])
        b1 = sbuf("b1", [P, NB1])
        b2 = sbuf("b2", [P, NB2])
        h1 = sbuf("h1", [P, NB1, CHUNK])
        h2 = sbuf("h2", [P, NB2, CHUNK])
        NH = N1 // TILES
        w1_in = [XP[:, :, :], h1[:, 0:KP, :]]
        w1d_in = [scratch[:, STAGES * VK * D:STAGES * VK * D + N1], h2[:, :, :].rearrange("p m b -> p (m b)")]
        ids_on_rows = h1[0:U, :, :].rearrange("u k b -> u (k b)").bitcast(fp16)
        y = sbuf("y", [1, CHUNK])
        ident = sbuf("ident", [P, P])
        ident16 = sbuf("ident16", [P, P], fp16)
        tbl = sbuf("tbl", [VP, U, PARTS, VK, D], fp32r)
        rows32 = sbuf("rows32", [VP, VK], i32)
        rows = sbuf("rows", [VP, VK], fp16)
        onehot = [sbuf(f"onehot{i}", [VP, VK, CHUNK], fp32r) for i in range(ONEHOTS)]

        Fps = psum("Fps", [P, MLP_BANK + 2, BANK])
        Hps = Fps[:, MLP_BANK:MLP_BANK + 2, :]
        Gps = psum("Gps", [P, 2, BANKS, BANK])

        idx_landed = [sem(f"idx_landed{h}") for h in range(TILES)]
        later_ids_landed = sem("later_ids_landed")
        later_ids_ready = sem("later_ids_ready")
        ids_turned = sem("ids_turned")
        ids_turned_out = sem("ids_turned_out")
        ids_in_dram = sem("ids_in_dram")
        spread_landed = sem("spread_landed")
        dense_landed = [sem(f"dense_landed{h}") for h in range(TILES)]
        x_landed = [[sem(f"x_landed{h}_{t}") for t in range(NT)] for h in range(TILES)]
        gathers_begun = sem("gathers_begun")
        tbl_landed = [sem(f"tbl_landed{i}") for i in range(STAGES)]
        tbl_hi = sem("tbl_hi")
        tbl_lo = sem("tbl_lo")
        w1_landed = [sem(f"w1_landed{i}") for i in range(2)]
        w1d_landed = sem("w1d_landed")
        w1_hi = sem("w1_hi")
        w1d_hi = sem("w1d_hi")
        w1_lo = sem("w1_lo")
        w1d_summed = sem("w1d_summed")
        mlp_landed = sem("mlp_landed")
        pads_zeroed = sem("pads_zeroed")
        consts = sem("consts")
        ident16_ready = sem("ident16_ready")
        rows_ready = sem("rows_ready")
        lidx16_ready = sem("lidx16_ready")
        spread = sem("spread")
        spread_out = sem("spread_out")
        onehot_ready = sem("onehot_ready")
        looked_up = sem("looked_up")
        transposed = sem("transposed")
        lookups_out = sem("lookups_out")
        transposes_out = sem("transposes_out")
        xd_hi = sem("xd_hi")
        xd_ready = sem("xd_ready")
        xp_hi = sem("xp_hi")
        xp_ready = sem("xp_ready")
        products_done = sem("products_done")
        pairs_dve = sem("pairs_dve")
        pairs_act = sem("pairs_act")
        packed = sem("packed")
        packed_last = [sem(f"packed_last{i}") for i in range(KP)]
        packed_by_pool = [sem(f"packed_by_pool{i}") for i in range(KP)]
        l1_done = sem("l1_done")
        h1_ready = sem("h1_ready")
        l2_done = sem("l2_done")
        h2_ready = sem("h2_ready")
        l3_done = sem("l3_done")
        y_ready = sem("y_ready")
        y_stored = sem("y_stored")

        def t_count(c, h, t):
            return (c * TILES + h) * NT + t + 1

        def p_count(c, h, k):
            return (c * TILES + h) * PGROUPS + k + 1

        def products_of_quadrant(c, h, k, q):
            b0 = h * P + k * PG_SAMPLES
            dst = I[0:G, :, b0:b0 + PG_SAMPLES].rearrange("p g (a m s) -> p a m s g", a=BANKS, m=MB)
            src = Gps[QUAD * q:QUAD * q + G, k % 2, :, 0:MB * SQ * G].rearrange(
                "p a (m s g) -> p a m s g", m=MB, s=SQ)
            return dst[:, :, :, q, :], src[:, :, :, q, :]

        def pack_piece(eng, piece):
            p, g, n, row = piece
            at = row % P
            return eng.dma_start(XP[at:at + n, row // P, :], I[p:p + 1, g - 1:g - 1 + n, :])

        def layer1_bank(c, n):
            return (MLP_BANK + n) % 4 if isinstance(c, int) and c == CHUNKS - 1 else MLP_BANK + n % 2

        block = ctx.enter_context(nc.Block())

        @block.sync
        def _(sp):
            def load_tile(c, h):
                part = bass.ds(sp.snap(c * CHUNK + h * P), P)
                sp.wait_ge(transposed, t_count(c - 1, h, NT - 1))
                sp.dma_start(idx[h][:, :], ids[part, :]).then_inc(idx_landed[h], 16)
                sp.dma_start(X[h][:, 0, :], dense[part, :]).then_inc(dense_landed[h], 16)

            def spread_lookup_indices(c):
                samples = bass.ds(sp.snap((c - 1) * CHUNK), CHUNK)
                sp.wait_ge(onehot_ready, c * U)
                sp.dma_start(lidx_all[0:VP, :, :], turned_ids[:, samples].partition_broadcast(VP)
                             ).then_inc(spread_landed, 16)

            def pack(c):
                sp.wait_ge(pairs_dve, p_count(c, 1, PGROUPS - 1))
                sp.wait_ge(pairs_act, p_count(c, 1, PGROUPS - 1))
                for piece in PACKS:
                    pack_piece(sp, piece).then_inc(packed, 16)

            def pack_last():
                sp.wait_ge(xp_ready, CHUNKS - 1)
                sp.wait_ge(pairs_dve, p_count(CHUNKS - 1, 1, PGROUPS - 1))
                sp.wait_ge(pairs_act, p_count(CHUNKS - 1, 1, PGROUPS - 1))
                for i in range(KP):
                    for piece in SP_PIECES[i]:
                        pack_piece(sp, piece).then_inc(packed_last[i], 16)

            for h in range(TILES):
                sp.dma_start(idx[h][:, :], ids[h * P:(h + 1) * P, :]).then_inc(idx_landed[h], 16)
            sp.dma_start(X[0][:, 0, :], dense[0:P, :]).then_inc(dense_landed[0], 16)
            for u in range(U):
                if u >= STAGES:
                    sp.wait_ge(tbl_lo, u - STAGES + 1)
                sp.dma_start(tbl32[u % STAGES], tables[LOOKUPS[u] - 1].rearrange("(p k) d -> p k d", k=VK)
                             ).then_inc(tbl_landed[u % STAGES], 16)
                if u == 1:
                    sp.dma_start(X[1][:, 0, :], dense[P:2 * P, :]).then_inc(dense_landed[1], 16)
                    sp.dma_start(later_ids[:, :, :], ids[CHUNK:B, :].rearrange("(t p) f -> p t f", p=P)
                                 ).then_inc(later_ids_landed, 16)
            for k in range(2):
                sp.dma_start(w1d_in[k], w_top1[k * (D + PAIRS):k * (D + PAIRS) + D, :]).then_inc(w1d_landed, 16)

            def load_w1(half):
                cols = slice(half * NH, (half + 1) * NH)
                sp.dma_start(w1_in[half][:, 0:KP - 1, :],
                             w_top1[D:D + (KP - 1) * P, cols].rearrange("(k p) n -> p k n", p=P)
                             ).then_inc(w1_landed[half], 16)
                sp.dma_start(w1_in[half][0:k_rows(KP - 1), KP - 1, :], w_top1[D + (KP - 1) * P:D + PAIRS, cols]
                             ).then_inc(w1_landed[half], 16)

            load_w1(0)
            sp.dma_start(W2[:, :, :], w_top2.rearrange("(k p) n -> p k n", p=P)).then_inc(mlp_landed, 16)
            with nc.allow_non_contiguous_dma(reason="1024 values in all, once"):
                sp.dma_start(b1[:, :], b_top1.rearrange("(k p) -> p k", p=P)).then_inc(mlp_landed, 16)
                sp.dma_start(b2[:, :], b_top2.rearrange("(k p) -> p k", p=P)).then_inc(mlp_landed, 16)
                sp.dma_start(W3[:, :], w_top3.rearrange("(k p) o -> p (k o)", p=P)).then_inc(mlp_landed, 16)

            sp.wait_ge(ids_turned_out, len(TURNS))
            sp.dma_start(turned_ids, ids_on_rows[:, 0:B - CHUNK]).then_inc(ids_in_dram, 16)
            load_tile(1, 0)
            sp.wait_ge(ids_in_dram, 16)
            spread_lookup_indices(1)
            load_w1(1)
            load_tile(1, 1)
            with sp.Fori(1, CHUNKS - 1) as c:
                pack(c - 1)
                spread_lookup_indices(c + 1)
                load_tile(c + 1, 0)
                load_tile(c + 1, 1)
            pack(CHUNKS - 2)
            pack_last()

        @block.gpsimd
        def _(pool):
            pool.memset(ident[:, :], 0.0).then_inc(consts, 1)
            pool.iota(rows32[:, :], pattern=[[1, VK]], base=0, channel_multiplier=VK).then_inc(consts, 1)
            pool.wait_ge(consts, 2)
            pool.affine_select(out=ident[:, :], in_=ident[:, :], compare_op=ALU.not_equal, fill=1.0,
                               base=0, pattern=[[-1, P]], channel_multiplier=1).then_inc(consts, 1)

            def gather_tile(c, h):
                pool.wait_ge(idx_landed[h], (c + 1) * 16)
                pool.sem_inc(gathers_begun, 1)
                for t, slots in enumerate(TGROUPS):
                    for s in slots:
                        if s:
                            pool.indirect_dma_start(
                                X[h][:, XSLOTS.index(s), :], None, tables[s - 1][:, :],
                                bass.IndirectOffsetOnAxis(idx[h][:, s - 1:s], 0)).then_inc(x_landed[h][t], 16)

            gather_tile(0, 0)
            gather_tile(0, 1)
            with pool.Fori(1, CHUNKS) as c:
                gather_tile(c, 0)
                gather_tile(c, 1)
            pool.wait_ge(xp_ready, CHUNKS - 1)
            pool.wait_ge(pairs_dve, p_count(CHUNKS - 1, 1, PGROUPS - 1))
            pool.wait_ge(pairs_act, p_count(CHUNKS - 1, 1, PGROUPS - 1))
            for i in range(KP):
                for piece in POOL_PIECES[i]:
                    pack_piece(pool, piece).then_inc(packed_by_pool[i], 16)

        @block.scalar
        def _(act):
            def indices_out():
                for o, us in enumerate(SGROUPS):
                    act.wait_ge(spread, o + 1)
                    n = len(us)
                    act.activation(lidx_all[:, us[0]:us[0] + n, :],
                                   Hps[:, o % 2, 0:n * CHUNK].rearrange("p (u b) -> p u b", u=n),
                                   ACT.Copy).then_inc(spread_out, 1)

            def later_indices_out():
                for o, ts in enumerate(TURNS):
                    act.wait_ge(ids_turned, o + 1)
                    act.activation(ids_on_rows[:, ts[0] * P:(ts[-1] + 1) * P],
                                   Hps[0:U, o % 2, 0:len(ts) * P], ACT.Copy).then_inc(ids_turned_out, 1)

            def lookup_out(c, u, first):
                if u == 0 and not first:
                    act.wait_ge(products_done, p_count(c - 1, 1, PGROUPS - 1))
                    act.wait_ge(xd_ready, c * TILES)
                act.wait_ge(looked_up, c * U + u + 1)
                src = Fps[:, FILL_BANK[FILL_ORDER.index(("lookup", u))], 0:CHUNK].rearrange("d (h b) -> d h b", h=TILES)
                act.activation(XT[:, :, :, LOOKUPS[u]], src, ACT.Copy).then_inc(lookups_out, 1)

            def transpose_out(c, h, t):
                act.wait_ge(transposed, t_count(c, h, t))
                slots = TGROUPS[t]
                act.activation(XT[:, h, :, step_slice(slots)],
                               Fps[:, FILL_BANK[FILL_ORDER.index((h, t))], 0:len(slots) * P].rearrange(
                                   "d (f b) -> d b f", f=len(slots)), ACT.Copy).then_inc(transposes_out, 1)

            def features_out(c, first=False, result=False):
                for kind, n in FEATURES:
                    if kind == "lookup":
                        lookup_out(c, n, first)
                        if result and n == 0:
                            result_out(c - 2)
                    else:
                        transpose_out(c, 0, n)

            def pairs_out(c, h, k):
                if h == 0 and k == 0 and not (isinstance(c, int) and c == 0):
                    act.wait_ge(packed, 16 * len(PACKS) * c)
                act.wait_ge(products_done, p_count(c, h, k))
                for q in ACT_QUADRANTS:
                    dst, src = products_of_quadrant(c, h, k, q)
                    last = act.activation(dst, src, ACT.Copy)
                last.then_inc(pairs_act, 1)

            def tile1_and_pairs_out(c):
                for what, n in MIXED:
                    if what == "transpose":
                        transpose_out(c, 1, n)
                    else:
                        pairs_out(c, 0, n)

            def layers_out(c):
                for n in range(NB1):
                    act.wait_ge(l1_done, c * NB1 + n + 1)
                    act.activation(h1[:, n, :], Fps[:, layer1_bank(c, n), 0:CHUNK], ACT.Relu, bias=b1[:, n:n + 1]
                                   ).then_inc(h1_ready, 1)
                for m in range(NB2):
                    act.wait_ge(l2_done, c * NB2 + m + 1)
                    act.activation(h2[:, m, :], Hps[:, m, 0:CHUNK], ACT.Relu, bias=b2[:, m:m + 1]
                                   ).then_inc(h2_ready, 1)
                if not (isinstance(c, int) and c == 0):
                    act.wait_ge(y_stored, c * 16)

            def result_out(c):
                fixed = isinstance(c, int)
                first_row = c * CHUNK if fixed else act.snap(c * CHUNK)
                act.wait_ge(l3_done, c + 1)
                act.activation(y[:, :], Hps[0:1, 0, 0:CHUNK], ACT.Copy).then_inc(y_ready, 1)
                act.wait_ge(y_ready, c + 1)
                act.dma_start(out[bass.ds(first_row, CHUNK), :].rearrange("b o -> o b"), y[:, :]
                              ).then_inc(y_stored, 16)

            def products_out(c):
                tile1_and_pairs_out(c)
                for k in range(PGROUPS):
                    pairs_out(c, 1, k)

            for u in range(U):
                act.wait_ge(tbl_landed[u % STAGES], 16 * (u // STAGES + 1))
                act.activation(tbl[:, u, 0, :, :], tbl32[u % STAGES], ACT.Copy).then_inc(tbl_hi, 1)
                if u == 0:
                    indices_out()
            features_out(0, True)
            later_indices_out()
            act.wait_ge(w1d_summed, 1)
            tile1_and_pairs_out(0)
            for half in range(2):
                act.wait_ge(w1_landed[half], 2 * 16)
                cols = slice(half * NH, (half + 1) * NH)
                for part in PAIR_BLOCKS:
                    act.activation(W1[part[0], 0, part[1], cols], w1_in[half][part], ACT.Copy).then_inc(w1_hi, 1)
            for k in range(PGROUPS):
                pairs_out(0, 1, k)
            features_out(1)
            products_out(1)
            act.wait_ge(mlp_landed, 4 * 16)
            layers_out(0)
            with act.Fori(2, CHUNKS) as c:
                features_out(c, result=True)
                products_out(c)
                layers_out(c - 1)
            result_out(CHUNKS - 2)
            layers_out(CHUNKS - 1)
            result_out(CHUNKS - 1)
            act.wait_ge(y_stored, CHUNKS * 16)

        @block.vector
        def _(dve):
            def one_hot(c, u, first=False):
                if first:
                    dve.wait_ge(spread_out, u // SG + 1)
                else:
                    dve.wait_ge(spread_landed, 16 * c)
                if not (first and u < ONEHOTS):
                    former, c0 = former_use([n % ONEHOTS for n in range(U)], u, c)
                    dve.wait_ge(looked_up, c0 * U + former + 1)
                index = lidx_all[0:VP, u:u + 1, :].to_broadcast([VP, VK, CHUNK])
                row = rows[:, :].unsqueeze(2).to_broadcast([VP, VK, CHUNK])
                dve.tensor_tensor(onehot[u % ONEHOTS][:, :, :], index, row, ALU.is_equal
                                  ).then_inc(onehot_ready, 1)

            def one_hots(c, first=False):
                for u in range(ONEHOTS, U):
                    one_hot(c, u, first)

            def dense_out(c, h, first=False):
                if h == 0 and not first:
                    dve.wait_ge(l1_done, c * NB1)
                dve.wait_ge(transposes_out, t_count(c, h, 0))
                x, samples = XT[:, h, :, 0], slice(h * P, (h + 1) * P)
                dve.tensor_copy(XD[:, 0, samples], x).then_inc(xd_hi, 1)
                dve.wait_ge(xd_hi, c * TILES + h + 1)
                dve.tensor_tensor(XD[:, 1, samples], x, XD[:, 0, samples], ALU.subtract).then_inc(xd_ready, 1)

            def split_pairs(c, first=False):
                dve.wait_ge(packed, 16 * len(PACKS) * (c + 1))
                if not first:
                    dve.wait_ge(l1_done, c * NB1)
                for rows_, steps in PAIR_BLOCKS:
                    dve.tensor_copy(XPR[rows_, 0, steps, :], XP[rows_, steps, :]).then_inc(xp_hi, 1)
                for n, (rows_, steps) in enumerate(PAIR_BLOCKS):
                    dve.wait_ge(xp_hi, c * len(PAIR_BLOCKS) + n + 1)
                    last = dve.tensor_tensor(XPR[rows_, 1, steps, :], XP[rows_, steps, :], XPR[rows_, 0, steps, :],
                                             ALU.subtract)
                last.then_inc(xp_ready, 1)

            def pairs_out(c, h, k):
                if h == 0 and k == 0 and not (isinstance(c, int) and c == 0):
                    dve.wait_ge(packed, 16 * len(PACKS) * c)
                dve.wait_ge(products_done, p_count(c, h, k))
                for q in DVE_QUADRANTS:
                    dst, src = products_of_quadrant(c, h, k, q)
                    last = dve.tensor_copy(dst, src)
                last.then_inc(pairs_dve, 1)

            def split_last_pairs():
                dve.wait_ge(l1_done, (CHUNKS - 1) * NB1)
                for i in range(KP):
                    dve.wait_ge(packed_last[i], 16 * len(SP_PIECES[i]))
                    dve.wait_ge(packed_by_pool[i], 16 * len(POOL_PIECES[i]))
                    pairs, parts = XP[0:k_rows(i), i, :], XPR[0:k_rows(i), :, i, :]
                    dve.tensor_copy(parts[:, 0, :], pairs).then_inc(xp_hi, 1)
                    dve.wait_ge(xp_hi, (CHUNKS - 1) * len(PAIR_BLOCKS) + i + 1)
                    dve.tensor_tensor(parts[:, 1, :], pairs, parts[:, 0, :], ALU.subtract).then_inc(xp_ready, 1)

            def tile_pairs_out(c, h):
                for k in range(PGROUPS):
                    pairs_out(c, h, k)

            def first_one_hots(c):
                for u in range(ONEHOTS):
                    one_hot(c, u)

            dve.memset(XT[:, :, :, F:QUAD], 0.0).then_inc(pads_zeroed, 1)
            dve.wait_ge(consts, 3)
            dve.tensor_copy(ident16[:, :], ident[:, :]).then_inc(ident16_ready, 1)
            for h in range(TILES):
                dve.wait_ge(idx_landed[h], 16)
                last = dve.tensor_copy(lidx16[:, h, :], idx[h][:, :])
            last.then_inc(lidx16_ready, 1)
            dve.tensor_copy(rows[:, :], rows32[:, :]).then_inc(rows_ready, 1)
            dve.wait_ge(rows_ready, 1)
            for u in range(U):
                dve.wait_ge(tbl_hi, u + 1)
                dve.tensor_tensor(tbl[:, u, 1, :, :], tbl32[u % STAGES], tbl[:, u, 0, :, :],
                                  ALU.subtract).then_inc(tbl_lo, 1)
                if u < ONEHOTS:
                    one_hot(0, u, True)
            one_hots(0, True)
            dve.wait_ge(later_ids_landed, 16)
            for u, n in ID_RUNS:
                f = LOOKUPS[u] - 1
                last = dve.tensor_copy(later_ids16[:, :, u:u + n], later_ids[:, :, f:f + n])
            last.then_inc(later_ids_ready, 1)
            dve.wait_ge(w1d_landed, 2 * 16)
            dve.tensor_tensor(w1d_in[1], w1d_in[0], w1d_in[1], ALU.add).then_inc(w1d_summed, 1)
            dve.wait_ge(w1d_summed, 1)
            tile_pairs_out(0, 0)
            dve.tensor_copy(W1D[:, 0, :], w1d_in[1]).then_inc(w1d_hi, 1)
            dve.wait_ge(w1d_hi, 1)
            dve.tensor_tensor(W1D[:, 1, :], w1d_in[1], W1D[:, 0, :], ALU.subtract).then_inc(w1_lo, 1)
            for half in range(2):
                cols = slice(half * NH, (half + 1) * NH)
                for n, part in enumerate(PAIR_BLOCKS):
                    dve.wait_ge(w1_hi, half * 2 + n + 1)
                    dve.tensor_tensor(W1[part[0], 1, part[1], cols], w1_in[half][part], W1[part[0], 0, part[1], cols],
                                      ALU.subtract).then_inc(w1_lo, 1)
            tile_pairs_out(0, 1)
            first_one_hots(1)
            dense_out(0, 0, True)
            dense_out(0, 1)

            def chunk_after_first_one_hots(c):
                one_hots(c)
                split_pairs(c - 1, first=isinstance(c, int) and c == 1)
                for h in range(TILES):
                    tile_pairs_out(c, h)

            chunk_after_first_one_hots(1)
            first_one_hots(2)
            for h in range(TILES):
                dense_out(1, h)
            with dve.Fori(2, CHUNKS - 1) as c:
                chunk_after_first_one_hots(c)
                first_one_hots(c + 1)
                for h in range(TILES):
                    dense_out(c, h)
            chunk_after_first_one_hots(CHUNKS - 1)
            for h in range(TILES):
                dense_out(CHUNKS - 1, h)
            split_last_pairs()

        @block.tensor
        def _(pe):
            def spread_indices():
                pe.wait_ge(lidx16_ready, 1)
                for o, us in enumerate(SGROUPS):
                    if o >= 2:
                        pe.wait_ge(spread_out, o - 1)
                    for u in us:
                        for h in range(TILES):
                            at = (u - us[0]) * CHUNK + h * P
                            index = lidx16[:, h, LOOKUPS[u] - 1:LOOKUPS[u]].to_broadcast([P, P])
                            last = pe.matmul(Hps[:, o % 2, at:at + P], index, ident16[:, :], start=True, stop=True)
                    last.then_inc(spread, 1)

            def turn_indices():
                pe.wait_ge(later_ids_ready, 1)
                pe.wait_ge(lookups_out, U)
                pe.wait_ge(transposes_out, NT)
                for o, ts in enumerate(TURNS):
                    if o >= 2:
                        pe.wait_ge(ids_turned_out, o - 1)
                    for n, t in enumerate(ts):
                        last = pe.matmul(Hps[0:U, o % 2, n * P:(n + 1) * P], later_ids16[:, t, :], ident16[:, :],
                                         start=True, stop=True)
                    last.then_inc(ids_turned, 1)

            def wait_for_bank(c, i):
                former, c0 = former_use(FILL_BANK, i, c)
                if isinstance(c0, int) and c0 < 0 and FILL_BANK[i] < MLP_BANK:
                    return
                kind, n = FILL_ORDER[former]
                if FILL_BANK[i] >= MLP_BANK and former > i:
                    if isinstance(c, int) and c == 0:
                        pe.wait_ge(spread_out, NS)
                    elif isinstance(c, int) and c == 1:
                        pe.wait_ge(ids_turned_out, len(TURNS))
                    else:
                        pe.wait_ge(y_ready, c - 1)
                elif kind == "lookup":
                    pe.wait_ge(lookups_out, c0 * U + n + 1)
                else:
                    pe.wait_ge(transposes_out, t_count(c0, kind, n))

            def look_up(c, u, first):
                i = FILL_ORDER.index(("lookup", u))
                wait_for_bank(c, i)
                pe.wait_ge(onehot_ready, c * U + u + 1)
                if first:
                    pe.wait_ge(tbl_lo, u + 1)
                for k in range(VK):
                    for part in range(PARTS):
                        last = pe.matmul(Fps[:, FILL_BANK[i], 0:CHUNK], tbl[:, u, part, k, :], onehot[u % ONEHOTS][:, k, :],
                                         start=(k == 0 and part == 0), stop=(k == VK - 1 and part == PARTS - 1))
                last.then_inc(looked_up, 1)

            def transpose_group(c, h, t):
                i = FILL_ORDER.index((h, t))
                slots = TGROUPS[t]
                if t == 0:
                    pe.wait_ge(dense_landed[h], 16 * (c + 1))
                pe.wait_ge(x_landed[h][t], 16 * sum(s > 0 for s in slots) * (c + 1))
                wait_for_bank(c, i)
                for n, s in enumerate(slots):
                    last = pe.transpose(Fps[:, FILL_BANK[i], n * P:(n + 1) * P], X[h][:, XSLOTS.index(s), :], ident[:, :])
                last.then_inc(transposed, 1)

            def features(c, first=False, with_result=False):
                for kind, n in FEATURES:
                    if kind == "lookup":
                        look_up(c, n, first)
                        if with_result and n == 0:
                            result(c - 2)
                    else:
                        transpose_group(c, 0, n)

            def products(c, h, k, first=False):
                if k == 0:
                    pe.wait_ge(lookups_out, (c + 1) * U)
                    pe.wait_ge(transposes_out, t_count(c, h, NT - 1))
                if not (first and k < 2):
                    pe.wait_ge(pairs_dve, p_count(c, h, k) - 2)
                    pe.wait_ge(pairs_act, p_count(c, h, k) - 2)
                for m in range(BANKS * MB):
                    b = k * PG_SAMPLES + m * SQ
                    at = (m % MB) * SQ * G
                    last = pe.matmul(Gps[:, k % 2, m // MB, at:at + SQ * G],
                                     XT[:, h, b:b + SQ, :], XT[:, h, b:b + SQ, 1:F], start=True, stop=True)
                last.then_inc(products_done, 1)

            def tile1_and_products(c, first=False):
                for what, n in MIXED:
                    if what == "transpose":
                        transpose_group(c, 1, n)
                    else:
                        products(c, 0, n, first)

            def layers(c):
                pe.wait_ge(xp_ready, c + 1)
                pe.wait_ge(xd_ready, (c + 1) * TILES)
                for n in range(NB1):
                    if n >= 2:
                        pe.wait_ge(h1_ready, c * NB1 + n - 1)
                    layer1_dense(c, n)
                    for i in range(KP):
                        last = layer1_pairs(c, n, i)
                    last.then_inc(l1_done, 1)
                layer2(c)

            def last_layers():
                c = CHUNKS - 1
                pe.wait_ge(xd_ready, (c + 1) * TILES)
                for n in range(NB1):
                    layer1_dense(c, n)
                for i in range(KP):
                    pe.wait_ge(xp_ready, c + i + 1)
                    for n in range(NB1):
                        last = layer1_pairs(c, n, i)
                        if i == KP - 1:
                            last.then_inc(l1_done, 1)
                layer2(c)

            def layer1_dense(c, n):
                cols = slice(n * P, (n + 1) * P)
                for wp, xp in PRODUCTS_OF_PARTS:
                    pe.matmul(Fps[:, layer1_bank(c, n), 0:CHUNK], W1D[:, wp, cols], XD[:, xp, :],
                              start=(wp == xp), stop=False)

            def layer1_pairs(c, n, i):
                cols, rows_ = slice(n * P, (n + 1) * P), slice(0, k_rows(i))
                for wp, xp in PRODUCTS_OF_PARTS:
                    last = pe.matmul(Fps[:, layer1_bank(c, n), 0:CHUNK], W1[rows_, wp, i, cols], XPR[rows_, xp, i, :],
                                     start=False, stop=(i == KP - 1 and xp == 1))
                return last

            def layer2(c):
                for m in range(NB2):
                    pe.wait_ge(h1_ready, (c + 1) * NB1 - (1 - m))
                    for k in range(NB1):
                        if m == 0 and k == NB1 - 1:
                            pe.wait_ge(h1_ready, (c + 1) * NB1)
                        last = pe.matmul(Hps[:, m, 0:CHUNK], W2[:, k, m * P:(m + 1) * P], h1[:, k, :],
                                         start=(k == 0), stop=(k == NB1 - 1))
                    last.then_inc(l2_done, 1)

            def result(c):
                pe.wait_ge(h2_ready, (c + 1) * NB2)
                for m in range(NB2):
                    last = pe.matmul(Hps[0:1, 0, 0:CHUNK], W3[:, m:m + 1], h2[:, m, :],
                                     start=(m == 0), stop=(m == NB2 - 1))
                last.then_inc(l3_done, 1)

            def chunk_products(c, first=False):
                tile1_and_products(c, first)
                for k in range(PGROUPS):
                    products(c, 1, k)

            pe.wait_ge(ident16_ready, 1)
            spread_indices()
            features(0, True)
            turn_indices()
            pe.wait_ge(pads_zeroed, 1)
            chunk_products(0, True)
            features(1)
            chunk_products(1)
            pe.wait_ge(w1_lo, 1 + 2 * len(PAIR_BLOCKS))
            pe.wait_ge(mlp_landed, 4 * 16)
            layers(0)
            with pe.Fori(2, CHUNKS) as c:
                features(c, with_result=True)
                chunk_products(c)
                layers(c - 1)
            result(CHUNKS - 2)
            pe.wait_ge(y_ready, CHUNKS - 1)
            last_layers()
            result(CHUNKS - 1)


_INS = (['r_dense_output', 'ids'] + [f'tbl_{i}' for i in range(SPARSE)]
        + ['W_top1', 'b_top1', 'W_top2', 'b_top2', 'W_top3'])


def kernel(**inputs):
    import numpy as _np
    import concourse.bacc as _bacc
    from concourse import mybir as _mybir
    from concourse.bass_utils import run_bass_kernel_spmd as _run

    nc = _bacc.Bacc("TRN2", target_bir_lowering=False, num_devices=1)
    arrays, args = {}, []
    for name in _INS:
        a = _np.ascontiguousarray(inputs[name])
        arrays[f"in_{name}_dram"] = a
        args.append(nc.dram_tensor(f"in_{name}_dram", a.shape, _mybir.dt.from_np(a.dtype), kind="ExternalInput").ap())
    out = nc.dram_tensor("out_0_dram", (B, 1), _mybir.dt.float32, kind="ExternalOutput").ap()
    dlrm_tower(nc, args[0], args[1], args[2:2 + SPARSE], *args[2 + SPARSE:], out)
    r = _run(nc, [arrays], core_ids=[0])
    return r.results[0]["out_0_dram"]
```

```python
import concourse.bass as bass
from concourse import mybir
from contextlib import ExitStack

P = 128
QUAD = 32
B, D = 2048, 128
SPARSE = 26
F = SPARSE + 1
PAIRS = F * (F - 1) // 2
G = F - 1
N1, N2 = 512, 256
TILES = 2
CHUNK = TILES * P
CHUNKS = B // CHUNK
BANK = 512

LOOKUPS = [17, 1, 2, 4, 5, 7, 10, 20]
EARLY, EARLY_CHUNKS = 1, 2
VOCAB, VK = 1000, 8
VP = VOCAB // VK
U = len(LOOKUPS)
PARTS = 2
PRODUCTS_OF_PARTS = [(0, 0), (1, 0), (0, 1)]
ONEHOTS = 2
HALVES = 2
SG = BANK // CHUNK
SGROUPS = [list(range(u, min(U, u + SG))) for u in range(0, U, SG)]
NS = len(SGROUPS)
ID_RUNS = []
for u in range(U):
    if u and LOOKUPS[u] == LOOKUPS[u - 1] + 1:
        ID_RUNS[-1][1] += 1
    else:
        ID_RUNS.append([u, 1])
LATER_TILES = B // P - TILES
TURNED = BANK // P
TURNS = [range(t, min(LATER_TILES, t + TURNED)) for t in range(0, LATER_TILES, TURNED)]

TGROUPS = [[0, 3, 6, 9], [8, 11, 14, 17], [12, 15, 18, 21], [13, 16, 19, 22], [23, 24, 25, 26]]
NT = len(TGROUPS)
XSLOTS = [s for slots in TGROUPS for s in slots]
assert sorted(XSLOTS + LOOKUPS[EARLY:]) == list(range(F)) and XSLOTS[0] == 0

FEATURES = [("lookup", EARLY), ("lookup", EARLY + 1)]
for n in range(max(NT, U - EARLY - 2)):
    FEATURES += [(0, n)] * (n < NT) + [("lookup", EARLY + n + 2)] * (EARLY + n + 2 < U)
EARLY_FEATURES = [("lookup", u) for u in range(EARLY)] + FEATURES
MLP_BANK = 2

SQ = P // QUAD
MB = 4
BANKS = 2
PG_SAMPLES = BANKS * MB * SQ
PGROUPS = P // PG_SAMPLES
DVE_QUADRANTS, ACT_QUADRANTS = (0, 1, 2), (3,)
MIXED = [("transpose", 0), ("transpose", 1)]
for n in range(max(NT - 2, PGROUPS)):
    MIXED += [("products", n)] * (n < PGROUPS) + [("transpose", n + 2)] * (n + 2 < NT)
KP = -(-PAIRS // P)
NB1, NB2 = N1 // P, N2 // P


def pairs_of(p):
    return F - 1 - p


def k_rows(i):
    return min(P, PAIRS - i * P)


def packs():
    filled, found = [0] * KP, []
    for p in range(F - 1):
        step = [i for i in range(KP) if filled[i] + pairs_of(p) <= k_rows(i)][0]
        found.append((p, step, filled[step]))
        filled[step] += pairs_of(p)
    return found


def weight_runs():
    runs, row = [], D
    for p, step, at in packs():
        if runs and runs[-1][2] == step and runs[-1][0] + runs[-1][1] == row:
            runs[-1][1] += pairs_of(p)
        else:
            runs.append([row, pairs_of(p), step, at])
        row += pairs_of(p)
    return runs


PACKS = packs()
WEIGHT_RUNS = weight_runs()
PAIR_BLOCKS = [(slice(0, P), slice(0, KP - 1)), (slice(0, k_rows(KP - 1)), slice(KP - 1, KP))]
POOL_PIECES = [[piece for n, piece in enumerate(PACKS) if piece[1] == i and n % 5 in (1, 3)] for i in range(KP)]
SP_PIECES = [[piece for n, piece in enumerate(PACKS) if piece[1] == i and n % 5 not in (1, 3)] for i in range(KP)]


def step_slice(slots):
    step = slots[1] - slots[0] if len(slots) > 1 else 1
    return slice(slots[0], slots[-1] + 1, step)


def is_early(c):
    return isinstance(c, int) and c < EARLY_CHUNKS


def features_of(c):
    return EARLY_FEATURES if is_early(c) else FEATURES


def fill_order(c):
    features = features_of(c)
    return (features + [(1, t) for t in range(NT)],
            [i % 4 for i in range(len(features))] + [t % 2 for t in range(NT)])


def bank_of(c, fill):
    order, banks = fill_order(c)
    return banks[order.index(fill)]


def lookups_of(c):
    return range(0 if is_early(c) else EARLY, U)


def transposed_slots(c, t):
    return [s for s in TGROUPS[t] if not (is_early(c) and s in LOOKUPS)]


def former_use(order, i, c):
    same = [n for n in range(len(order)) if order[n] == order[i]]
    before = [n for n in same if n < i]
    return (before[-1], c) if before else (same[-1], c - 1)


def dlrm_tower(nc, dense, ids, tables, w_top1, b_top1, w_top2, b_top2, w_top3, out):
    fp32 = mybir.dt.float32
    fp32r = mybir.dt.float32r
    fp16 = mybir.dt.float16
    i32 = mybir.dt.int32
    ALU = mybir.AluOpType
    ACT = mybir.ActivationFunctionType

    with ExitStack() as ctx:
        def sbuf(name, shape, dt=fp32):
            return ctx.enter_context(nc.sbuf_tensor(name, shape, dt))

        def psum(name, shape):
            return ctx.enter_context(nc.psum_tensor(name, shape, fp32))

        def sem(name):
            return ctx.enter_context(nc.semaphore(name))

        idx = [sbuf(f"idx{h}", [P, SPARSE], i32) for h in range(TILES)]
        lidx16 = sbuf("lidx16", [P, TILES, SPARSE], fp16)
        later_ids = sbuf("later_ids", [P, LATER_TILES, SPARSE], i32)
        later_ids16 = sbuf("later_ids16", [P, LATER_TILES, U], fp16)
        turned_ids = nc.dram_tensor("turned_ids", (U, B - CHUNK), fp16, kind="Internal").ap()
        lidx_all = sbuf("lidx_all", [P, U, CHUNK], fp16)
        X = [sbuf(f"X{h}", [P, len(XSLOTS), D]) for h in range(TILES)]
        XT = sbuf("XT", [D, TILES, P, QUAD])
        XD = sbuf("XD", [D, PARTS, CHUNK], fp32r)
        scratch = sbuf("scratch", [P, G * CHUNK])
        I = scratch[0:QUAD, :].rearrange("p (g b) -> p g b", g=G)
        STAGES = G * CHUNK // (VK * D)
        tbl32 = [scratch[0:VP, i * VK * D:(i + 1) * VK * D].rearrange("p (k d) -> p k d", k=VK)
                 for i in range(STAGES)]
        XP = sbuf("XP", [P, KP, CHUNK])
        pairs_or_table = sbuf("pairs_or_table", [P, PARTS * VK * D], fp32r)
        XPR = pairs_or_table[:, 0:PARTS * KP * CHUNK].rearrange("p (a k b) -> p a k b", a=PARTS, k=KP)
        early_tbl = pairs_or_table[0:VP, :].rearrange("p (a k d) -> p a k d", a=PARTS, k=VK)
        W1 = sbuf("W1", [P, PARTS, KP, N1], fp32r)
        W1D = sbuf("W1D", [D, PARTS, N1], fp32r)
        W2 = sbuf("W2", [P, PARTS, NB1, N2], fp32r)
        W3 = sbuf("W3", [P, NB2])
        b1 = sbuf("b1", [P, NB1])
        b2 = sbuf("b2", [P, NB2])
        h1 = sbuf("h1", [P, 2, CHUNK])
        H1R = sbuf("H1R", [P, PARTS, NB1, CHUNK], fp32r)
        h2 = sbuf("h2", [P, NB2, CHUNK])

        def weight_stage(stage, blocks, cols):
            at = stage * VK * D
            return scratch[:, at:at + blocks * cols].rearrange("p (k n) -> p k n", k=blocks)

        W1D_STAGE, W1_STAGE, W2_STAGE = 2, 3, 5
        w1d_in = weight_stage(W1D_STAGE, 2, N1)
        w1_in = weight_stage(W1_STAGE, KP, N1)
        w2_in = weight_stage(W2_STAGE, NB1, N2)
        ids_on_rows = scratch[2 * QUAD:2 * QUAD + U, 0:VK * D].bitcast(fp16)
        y = sbuf("y", [1, CHUNK])
        ident = sbuf("ident", [P, P])
        ident16 = sbuf("ident16", [P, P], fp16)
        tbl = sbuf("tbl", [VP, U - EARLY, PARTS, VK, D], fp32r)
        rows32 = sbuf("rows32", [VP, VK], i32)
        rows = sbuf("rows", [VP, VK], fp16)
        onehot = [sbuf(f"onehot{i}", [VP, VK, CHUNK], fp32r) for i in range(ONEHOTS)]

        Fps = psum("Fps", [P, MLP_BANK + 2, BANK])
        Hps = Fps[:, MLP_BANK:MLP_BANK + 2, :]
        Gps = psum("Gps", [P, 2, BANKS, BANK])

        idx_landed = [sem(f"idx_landed{h}") for h in range(TILES)]
        later_ids_landed = sem("later_ids_landed")
        later_ids_ready = sem("later_ids_ready")
        ids_turned = sem("ids_turned")
        ids_turned_out = sem("ids_turned_out")
        ids_in_dram = sem("ids_in_dram")
        spread_landed = sem("spread_landed")
        dense_landed = [sem(f"dense_landed{h}") for h in range(TILES)]
        x_landed = [[sem(f"x_landed{h}_{t}") for t in range(NT)] for h in range(TILES)]
        gathers_begun = sem("gathers_begun")
        tbl_landed = [sem(f"tbl_landed{i}") for i in range(STAGES)]
        tbl_hi = sem("tbl_hi")
        tbl_lo = sem("tbl_lo")
        w1_landed = sem("w1_landed")
        w1d_landed = sem("w1d_landed")
        w1_hi = sem("w1_hi")
        w1d_hi = sem("w1d_hi")
        w1_lo = sem("w1_lo")
        w1d_summed = sem("w1d_summed")
        w2_landed = sem("w2_landed")
        w2_hi = sem("w2_hi")
        w2_lo = sem("w2_lo")
        mlp_landed = sem("mlp_landed")
        pads_zeroed = sem("pads_zeroed")
        consts = sem("consts")
        ident16_ready = sem("ident16_ready")
        pair_rowsready = sem("pair_rowsready")
        lidx16_ready = sem("lidx16_ready")
        spread = sem("spread")
        spread_out = sem("spread_out")
        onehot_ready = sem("onehot_ready")
        looked_up = sem("looked_up")
        transposed = sem("transposed")
        lookups_out = sem("lookups_out")
        transposes_out = sem("transposes_out")
        xd_hi = sem("xd_hi")
        xd_ready = sem("xd_ready")
        xp_hi = sem("xp_hi")
        xp_ready = sem("xp_ready")
        products_done = sem("products_done")
        pairs_dve = sem("pairs_dve")
        pairs_act = sem("pairs_act")
        packed = sem("packed")
        packed_last = [sem(f"packed_last{i}") for i in range(KP)]
        packed_by_pool = [sem(f"packed_by_pool{i}") for i in range(KP)]
        l1_done = sem("l1_done")
        h1_hi = sem("h1_hi")
        h1_out = sem("h1_out")
        h1_lo = sem("h1_lo")
        l2_done = sem("l2_done")
        h2_ready = sem("h2_ready")
        l3_done = sem("l3_done")
        y_ready = sem("y_ready")
        y_stored = sem("y_stored")

        def is_last(c):
            return isinstance(c, int) and c == CHUNKS - 1

        def layer2_out(c, m):
            return Gps[:, 0, m, 0:CHUNK] if is_last(c) else Hps[:, m, 0:CHUNK]

        def onehot_buffer(u):
            return (u - EARLY) % ONEHOTS

        def table(u):
            return early_tbl if u < EARLY else tbl[:, u - EARLY, :, :, :]

        def l_count(c, u):
            if isinstance(c, int) and c < EARLY_CHUNKS:
                return c * U + u + 1
            return c * (U - EARLY) + (EARLY_CHUNKS - 1) * EARLY + u + 1

        def l_end(c):
            return c * (U - EARLY) + (EARLY_CHUNKS - 1) * EARLY + U if not is_early(c) else (c + 1) * U

        def x_count(c, t):
            always = [s for s in TGROUPS[t] if s and s not in LOOKUPS]
            later = [s for s in TGROUPS[t] if s in LOOKUPS]
            return len(always) * (c + 1) + (0 if is_early(c) else len(later) * (c + 1 - EARLY_CHUNKS))

        def t_count(c, h, t):
            return (c * TILES + h) * NT + t + 1

        def p_count(c, h, k):
            return (c * TILES + h) * PGROUPS + k + 1

        def products_of_quadrant(c, h, k, q):
            b0 = h * P + k * PG_SAMPLES
            dst = I[0:G, :, b0:b0 + PG_SAMPLES].rearrange("p g (a m s) -> p a m s g", a=BANKS, m=MB)
            src = Gps[QUAD * q:QUAD * q + G, k % 2, :, 0:MB * SQ * G].rearrange(
                "p a (m s g) -> p a m s g", m=MB, s=SQ)
            return dst[:, :, :, q, :], src[:, :, :, q, :]

        def pack_piece(eng, piece):
            p, step, at = piece
            return eng.dma_start(XP[at:at + pairs_of(p), step, :], I[p:p + 1, p:G, :])

        def layer1_bank(c, n):
            return (MLP_BANK + n) % 4 if is_last(c) else MLP_BANK + n % 2

        block = ctx.enter_context(nc.Block())

        @block.sync
        def _(sp):
            def load_tile(c, h):
                part = bass.ds(sp.snap(c * CHUNK + h * P), P)
                sp.wait_ge(transposed, t_count(c - 1, h, NT - 1))
                sp.dma_start(idx[h][:, :], ids[part, :]).then_inc(idx_landed[h], 16)
                sp.dma_start(X[h][:, 0, :], dense[part, :]).then_inc(dense_landed[h], 16)

            def spread_lookup_indices(c):
                samples = bass.ds(sp.snap((c - 1) * CHUNK), CHUNK)
                sp.wait_ge(onehot_ready, HALVES * l_end(c - 1))
                us = slice(lookups_of(c)[0], U)
                sp.dma_start(lidx_all[0:VP, us, :], turned_ids[us, samples].partition_broadcast(VP)
                             ).then_inc(spread_landed, 16)

            def pack(c):
                sp.wait_ge(pairs_dve, p_count(c, 1, PGROUPS - 1))
                sp.wait_ge(pairs_act, p_count(c, 1, PGROUPS - 1))
                for piece in PACKS:
                    pack_piece(sp, piece).then_inc(packed, 16)

            def pack_last():
                sp.wait_ge(xp_ready, CHUNKS - 1)
                sp.wait_ge(pairs_dve, p_count(CHUNKS - 1, 1, PGROUPS - 1))
                sp.wait_ge(pairs_act, p_count(CHUNKS - 1, 1, PGROUPS - 1))
                for i in range(KP):
                    for piece in SP_PIECES[i]:
                        pack_piece(sp, piece).then_inc(packed_last[i], 16)

            for h in range(TILES):
                sp.dma_start(idx[h][:, :], ids[h * P:(h + 1) * P, :]).then_inc(idx_landed[h], 16)
            sp.dma_start(X[0][:, 0, :], dense[0:P, :]).then_inc(dense_landed[0], 16)
            for u in range(U):
                if u >= STAGES:
                    sp.wait_ge(tbl_lo, u - STAGES + 1)
                sp.dma_start(tbl32[u % STAGES], tables[LOOKUPS[u] - 1].rearrange("(p k) d -> p k d", k=VK)
                             ).then_inc(tbl_landed[u % STAGES], 16)
                if u == 1:
                    sp.dma_start(X[1][:, 0, :], dense[P:2 * P, :]).then_inc(dense_landed[1], 16)
                    sp.dma_start(later_ids[:, :, :], ids[CHUNK:B, :].rearrange("(t p) f -> p t f", p=P)
                                 ).then_inc(later_ids_landed, 16)
            with nc.allow_non_contiguous_dma(reason="1024 values in all, once"):
                sp.dma_start(b1[:, :], b_top1.rearrange("(k p) -> p k", p=P)).then_inc(mlp_landed, 16)
                sp.dma_start(b2[:, :], b_top2.rearrange("(k p) -> p k", p=P)).then_inc(mlp_landed, 16)
                sp.dma_start(W3[:, :], w_top3.rearrange("(k p) o -> p (k o)", p=P)).then_inc(mlp_landed, 16)
            sp.wait_ge(tbl_lo, W1D_STAGE + 1)
            sp.dma_start(w1d_in[:, 0, :], w_top1[0:D, :]).then_inc(w1d_landed, 16)
            sp.dma_start(w1d_in[:, 1, :], w_top1[D + PAIRS:2 * D + PAIRS, :]).then_inc(w1d_landed, 16)
            sp.wait_ge(tbl_lo, W1_STAGE + 2)
            for row, n, step, at in WEIGHT_RUNS:
                sp.dma_start(w1_in[at:at + n, step, :], w_top1[row:row + n, :]).then_inc(w1_landed, 16)
            sp.wait_ge(tbl_lo, W2_STAGE + 1)
            sp.dma_start(w2_in, w_top2.rearrange("(k p) n -> p k n", p=P)).then_inc(w2_landed, 16)

            sp.wait_ge(ids_turned_out, len(TURNS))
            sp.dma_start(turned_ids, ids_on_rows[:, 0:B - CHUNK]).then_inc(ids_in_dram, 16)
            load_tile(1, 0)
            sp.wait_ge(ids_in_dram, 16)
            spread_lookup_indices(1)
            load_tile(1, 1)
            with sp.Fori(1, CHUNKS - 1) as c:
                pack(c - 1)
                spread_lookup_indices(c + 1)
                load_tile(c + 1, 0)
                load_tile(c + 1, 1)
            pack(CHUNKS - 2)
            pack_last()

        @block.gpsimd
        def _(pool):
            pool.memset(ident[:, :], 0.0).then_inc(consts, 1)
            pool.iota(rows32[:, :], pattern=[[1, VK]], base=0, channel_multiplier=VK).then_inc(consts, 1)
            pool.wait_ge(consts, 2)
            pool.affine_select(out=ident[:, :], in_=ident[:, :], compare_op=ALU.not_equal, fill=1.0,
                               base=0, pattern=[[-1, P]], channel_multiplier=1).then_inc(consts, 1)

            def gather_tile(c, h):
                pool.wait_ge(idx_landed[h], (c + 1) * 16)
                pool.sem_inc(gathers_begun, 1)
                for t in range(NT):
                    for s in transposed_slots(c, t):
                        if s:
                            pool.indirect_dma_start(
                                X[h][:, XSLOTS.index(s), :], None, tables[s - 1][:, :],
                                bass.IndirectOffsetOnAxis(idx[h][:, s - 1:s], 0)).then_inc(x_landed[h][t], 16)

            for c in range(EARLY_CHUNKS):
                gather_tile(c, 0)
                gather_tile(c, 1)
            with pool.Fori(EARLY_CHUNKS, CHUNKS) as c:
                gather_tile(c, 0)
                gather_tile(c, 1)
            pool.wait_ge(xp_ready, CHUNKS - 1)
            pool.wait_ge(pairs_dve, p_count(CHUNKS - 1, 1, PGROUPS - 1))
            pool.wait_ge(pairs_act, p_count(CHUNKS - 1, 1, PGROUPS - 1))
            for i in range(KP):
                for piece in POOL_PIECES[i]:
                    pack_piece(pool, piece).then_inc(packed_by_pool[i], 16)

        @block.scalar
        def _(act):
            def indices_out(groups):
                for us in groups:
                    o = SGROUPS.index(us)
                    act.wait_ge(spread, o + 1)
                    n = len(us)
                    act.activation(lidx_all[:, us[0]:us[0] + n, :],
                                   Hps[:, o % 2, 0:n * CHUNK].rearrange("p (u b) -> p u b", u=n),
                                   ACT.Copy).then_inc(spread_out, 1)

            def later_indices_out():
                for o, ts in enumerate(TURNS):
                    act.wait_ge(ids_turned, o + 1)
                    act.activation(ids_on_rows[:, ts[0] * P:(ts[-1] + 1) * P],
                                   Hps[0:U, o % 2, 0:len(ts) * P], ACT.Copy).then_inc(ids_turned_out, 1)

            def lookup_out(c, u, first):
                if u == lookups_of(c)[0] and not first:
                    act.wait_ge(products_done, p_count(c - 1, 1, PGROUPS - 1))
                    act.wait_ge(xd_ready, c * TILES)
                act.wait_ge(looked_up, HALVES * l_count(c, u))
                src = Fps[:, bank_of(c, ("lookup", u)), 0:CHUNK].rearrange("d (h b) -> d h b", h=TILES)
                act.activation(XT[:, :, :, LOOKUPS[u]], src, ACT.Copy).then_inc(lookups_out, 1)

            def transpose_out(c, h, t):
                act.wait_ge(transposed, t_count(c, h, t))
                slots = transposed_slots(c, t)
                act.activation(XT[:, h, :, step_slice(slots)],
                               Fps[:, bank_of(c, (h, t)), 0:len(slots) * P].rearrange(
                                   "d (f b) -> d b f", f=len(slots)), ACT.Copy).then_inc(transposes_out, 1)

            def features_out(c, first=False, result=False):
                for kind, n in features_of(c):
                    if kind == "lookup":
                        lookup_out(c, n, first)
                        if result and n == EARLY:
                            result_out(c - 2)
                    else:
                        transpose_out(c, 0, n)

            def pairs_out(c, h, k):
                if h == 0 and k == 0 and not (isinstance(c, int) and c == 0):
                    act.wait_ge(packed, 16 * len(PACKS) * c)
                act.wait_ge(products_done, p_count(c, h, k))
                for q in ACT_QUADRANTS:
                    dst, src = products_of_quadrant(c, h, k, q)
                    last = act.activation(dst, src, ACT.Copy)
                last.then_inc(pairs_act, 1)

            def tile1_and_pairs_out(c):
                for what, n in MIXED:
                    if what == "transpose":
                        transpose_out(c, 1, n)
                    else:
                        pairs_out(c, 0, n)

            def layers_out(c):
                def higher_part(n):
                    act.wait_ge(l1_done, c * NB1 + n + 1)
                    act.activation(H1R[:, 0, n, :], Fps[:, layer1_bank(c, n), 0:CHUNK], ACT.Relu,
                                   bias=b1[:, n:n + 1]).then_inc(h1_hi, 1)

                def whole(n):
                    if not (isinstance(c, int) and c == 0 and n < 2):
                        act.wait_ge(h1_lo, c * NB1 + n - 1)
                    act.activation(h1[:, n % 2, :], Fps[:, layer1_bank(c, n), 0:CHUNK], ACT.Relu,
                                   bias=b1[:, n:n + 1]).then_inc(h1_out, 1)

                if is_last(c):
                    for n in range(NB1):
                        higher_part(n)
                    for n in range(NB1):
                        whole(n)
                else:
                    for n in range(NB1):
                        higher_part(n)
                        whole(n)
                for m in range(NB2):
                    act.wait_ge(l2_done, c * NB2 + m + 1)
                    act.activation(h2[:, m, :], layer2_out(c, m), ACT.Relu, bias=b2[:, m:m + 1]
                                   ).then_inc(h2_ready, 1)
                if not (isinstance(c, int) and c == 0):
                    act.wait_ge(y_stored, c * 16)

            def result_out(c):
                fixed = isinstance(c, int)
                first_row = c * CHUNK if fixed else act.snap(c * CHUNK)
                act.wait_ge(l3_done, c + 1)
                act.activation(y[:, :], Hps[0:1, 0, 0:CHUNK], ACT.Copy).then_inc(y_ready, 1)
                act.wait_ge(y_ready, c + 1)
                act.dma_start(out[bass.ds(first_row, CHUNK), :].rearrange("b o -> o b"), y[:, :]
                              ).then_inc(y_stored, 16)

            def products_out(c):
                tile1_and_pairs_out(c)
                for k in range(PGROUPS):
                    pairs_out(c, 1, k)

            indices_out(SGROUPS[:2])
            for u in range(U):
                act.wait_ge(tbl_landed[u % STAGES], 16 * (u // STAGES + 1))
                act.activation(table(u)[:, 0, :, :], tbl32[u % STAGES], ACT.Copy).then_inc(tbl_hi, 1)
                if u == 0:
                    indices_out(SGROUPS[2:])
            features_out(0, True)
            later_indices_out()
            act.wait_ge(w1_lo, 1 + len(PAIR_BLOCKS))
            act.wait_ge(w2_lo, 1)
            tile1_and_pairs_out(0)
            for k in range(PGROUPS):
                pairs_out(0, 1, k)
            features_out(1)
            products_out(1)
            act.wait_ge(mlp_landed, 3 * 16)
            layers_out(0)
            with act.Fori(2, CHUNKS) as c:
                features_out(c, result=True)
                products_out(c)
                layers_out(c - 1)
            result_out(CHUNKS - 2)
            layers_out(CHUNKS - 1)
            result_out(CHUNKS - 1)
            act.wait_ge(y_stored, CHUNKS * 16)

        @block.vector
        def _(dve):
            def half_one_hot(c, u, half, first=False):
                if first:
                    dve.wait_ge(spread_out, u // SG + 1)
                else:
                    dve.wait_ge(spread_landed, 16 * c)
                us = lookups_of(c)
                if not (first and u < ONEHOTS):
                    former, c0 = former_use([onehot_buffer(n) for n in us], u - us[0], c)
                    dve.wait_ge(looked_up, HALVES * l_count(c0, us[0] + former) - (HALVES - 1 - half))
                nk = VK // HALVES
                ks = slice(half * nk, (half + 1) * nk)
                index = lidx_all[0:VP, u:u + 1, :].to_broadcast([VP, nk, CHUNK])
                row = rows[:, ks].unsqueeze(2).to_broadcast([VP, nk, CHUNK])
                dve.tensor_tensor(onehot[onehot_buffer(u)][:, ks, :], index, row, ALU.is_equal
                                  ).then_inc(onehot_ready, 1)

            def one_hot(c, u, first=False):
                for half in range(HALVES):
                    half_one_hot(c, u, half, first)

            def one_hots(c):
                for u in lookups_of(c)[ONEHOTS:]:
                    one_hot(c, u)

            def dense_out(c, h, first=False):
                if h == 0 and not first:
                    dve.wait_ge(l1_done, c * NB1)
                dve.wait_ge(transposes_out, t_count(c, h, 0))
                x, samples = XT[:, h, :, 0], slice(h * P, (h + 1) * P)
                dve.tensor_copy(XD[:, 0, samples], x).then_inc(xd_hi, 1)
                dve.wait_ge(xd_hi, c * TILES + h + 1)
                dve.tensor_tensor(XD[:, 1, samples], x, XD[:, 0, samples], ALU.subtract).then_inc(xd_ready, 1)

            def split_pairs(c, first=False):
                dve.wait_ge(packed, 16 * len(PACKS) * (c + 1))
                if first:
                    dve.wait_ge(looked_up, HALVES * l_count(EARLY_CHUNKS - 1, EARLY - 1))
                else:
                    dve.wait_ge(l1_done, c * NB1)
                for pair_rows, steps in PAIR_BLOCKS:
                    dve.tensor_copy(XPR[pair_rows, 0, steps, :], XP[pair_rows, steps, :]).then_inc(xp_hi, 1)
                for n, (pair_rows, steps) in enumerate(PAIR_BLOCKS):
                    dve.wait_ge(xp_hi, c * len(PAIR_BLOCKS) + n + 1)
                    last = dve.tensor_tensor(XPR[pair_rows, 1, steps, :], XP[pair_rows, steps, :],
                                             XPR[pair_rows, 0, steps, :],
                                             ALU.subtract)
                last.then_inc(xp_ready, 1)

            def pairs_out(c, h, k):
                if h == 0 and k == 0 and not (isinstance(c, int) and c == 0):
                    dve.wait_ge(packed, 16 * len(PACKS) * c)
                dve.wait_ge(products_done, p_count(c, h, k))
                for q in DVE_QUADRANTS:
                    dst, src = products_of_quadrant(c, h, k, q)
                    last = dve.tensor_copy(dst, src)
                last.then_inc(pairs_dve, 1)

            def split_last_pairs():
                dve.wait_ge(l1_done, (CHUNKS - 1) * NB1)
                for i in range(KP):
                    dve.wait_ge(packed_last[i], 16 * len(SP_PIECES[i]))
                    dve.wait_ge(packed_by_pool[i], 16 * len(POOL_PIECES[i]))
                    pairs, parts = XP[0:k_rows(i), i, :], XPR[0:k_rows(i), :, i, :]
                    dve.tensor_copy(parts[:, 0, :], pairs).then_inc(xp_hi, 1)
                    dve.wait_ge(xp_hi, (CHUNKS - 1) * len(PAIR_BLOCKS) + i + 1)
                    dve.tensor_tensor(parts[:, 1, :], pairs, parts[:, 0, :], ALU.subtract).then_inc(xp_ready, 1)

            def tile_pairs_out(c, h):
                for k in range(PGROUPS):
                    pairs_out(c, h, k)

            def layer1_parts(c, n):
                dve.wait_ge(h1_out, c * NB1 + n + 1)
                dve.tensor_tensor(H1R[:, 1, n, :], h1[:, n % 2, :], H1R[:, 0, n, :], ALU.subtract).then_inc(h1_lo, 1)

            def first_one_hots_and_layer1_parts(c):
                u0, u1 = lookups_of(c)[:ONEHOTS]
                half_one_hot(c, u0, 0)
                half_one_hot(c, u0, 1)
                layer1_parts(c - 2, 0)
                layer1_parts(c - 2, 1)
                half_one_hot(c, u1, 0)
                layer1_parts(c - 2, 2)
                half_one_hot(c, u1, 1)
                layer1_parts(c - 2, 3)

            dve.memset(XT[:, :, :, F:QUAD], 0.0).then_inc(pads_zeroed, 1)
            dve.wait_ge(consts, 3)
            dve.tensor_copy(ident16[:, :], ident[:, :]).then_inc(ident16_ready, 1)
            for h in range(TILES):
                dve.wait_ge(idx_landed[h], 16)
                last = dve.tensor_copy(lidx16[:, h, :], idx[h][:, :])
            last.then_inc(lidx16_ready, 1)
            dve.tensor_copy(rows[:, :], rows32[:, :]).then_inc(pair_rowsready, 1)
            dve.wait_ge(pair_rowsready, 1)
            for u in range(U):
                one_hot(0, u, True)
                dve.wait_ge(tbl_hi, u + 1)
                dve.tensor_tensor(table(u)[:, 1, :, :], tbl32[u % STAGES], table(u)[:, 0, :, :],
                                  ALU.subtract).then_inc(tbl_lo, 1)
            dve.wait_ge(later_ids_landed, 16)
            for u, n in ID_RUNS:
                f = LOOKUPS[u] - 1
                last = dve.tensor_copy(later_ids16[:, :, u:u + n], later_ids[:, :, f:f + n])
            last.then_inc(later_ids_ready, 1)
            dve.wait_ge(w1d_landed, 2 * 16)
            dve.tensor_tensor(w1d_in[:, 0, :], w1d_in[:, 0, :], w1d_in[:, 1, :], ALU.add).then_inc(w1d_summed, 1)
            dve.wait_ge(w1_landed, 16 * len(WEIGHT_RUNS))
            for pair_rows, steps in PAIR_BLOCKS:
                dve.tensor_copy(W1[pair_rows, 0, steps, :], w1_in[pair_rows, steps, :]).then_inc(w1_hi, 1)
            dve.wait_ge(w1d_summed, 1)
            dve.tensor_copy(W1D[:, 0, :], w1d_in[:, 0, :]).then_inc(w1d_hi, 1)
            for n, (pair_rows, steps) in enumerate(PAIR_BLOCKS):
                dve.wait_ge(w1_hi, n + 1)
                dve.tensor_tensor(W1[pair_rows, 1, steps, :], w1_in[pair_rows, steps, :], W1[pair_rows, 0, steps, :],
                                  ALU.subtract).then_inc(w1_lo, 1)
            dve.wait_ge(w1d_hi, 1)
            dve.tensor_tensor(W1D[:, 1, :], w1d_in[:, 0, :], W1D[:, 0, :], ALU.subtract).then_inc(w1_lo, 1)
            dve.wait_ge(w2_landed, 16)
            dve.tensor_copy(W2[:, 0, :, :], w2_in).then_inc(w2_hi, 1)
            dve.wait_ge(w2_hi, 1)
            dve.tensor_tensor(W2[:, 1, :, :], w2_in, W2[:, 0, :, :], ALU.subtract).then_inc(w2_lo, 1)
            dve.wait_ge(w1_lo, 1 + len(PAIR_BLOCKS))
            dve.wait_ge(w2_lo, 1)
            for k in range(PGROUPS):
                pairs_out(0, 0, k)
                if k in (1, 2):
                    one_hot(1, k - 1)
            tile_pairs_out(0, 1)
            dense_out(0, 0, True)
            dense_out(0, 1)

            def chunk_after_first_one_hots(c):
                one_hots(c)
                split_pairs(c - 1, first=isinstance(c, int) and c == 1)
                for h in range(TILES):
                    tile_pairs_out(c, h)

            chunk_after_first_one_hots(1)
            first_one_hots_and_layer1_parts(2)
            for h in range(TILES):
                dense_out(1, h)
            with dve.Fori(2, CHUNKS - 1) as c:
                chunk_after_first_one_hots(c)
                first_one_hots_and_layer1_parts(c + 1)
                for h in range(TILES):
                    dense_out(c, h)
            chunk_after_first_one_hots(CHUNKS - 1)
            for n in range(NB1):
                layer1_parts(CHUNKS - 2, n)
            for h in range(TILES):
                dense_out(CHUNKS - 1, h)
            split_last_pairs()
            for n in range(NB1):
                layer1_parts(CHUNKS - 1, n)

        @block.tensor
        def _(pe):
            def spread_indices():
                pe.wait_ge(lidx16_ready, 1)
                for o, us in enumerate(SGROUPS):
                    if o >= 2:
                        pe.wait_ge(spread_out, o - 1)
                    for u in us:
                        for h in range(TILES):
                            at = (u - us[0]) * CHUNK + h * P
                            index = lidx16[:, h, LOOKUPS[u] - 1:LOOKUPS[u]].to_broadcast([P, P])
                            last = pe.matmul(Hps[:, o % 2, at:at + P], index, ident16[:, :], start=True, stop=True)
                    last.then_inc(spread, 1)

            def turn_indices():
                pe.wait_ge(later_ids_ready, 1)
                pe.wait_ge(lookups_out, l_end(0))
                pe.wait_ge(transposes_out, NT)
                for o, ts in enumerate(TURNS):
                    if o >= 2:
                        pe.wait_ge(ids_turned_out, o - 1)
                    for n, t in enumerate(ts):
                        last = pe.matmul(Hps[0:U, o % 2, n * P:(n + 1) * P], later_ids16[:, t, :], ident16[:, :],
                                         start=True, stop=True)
                    last.then_inc(ids_turned, 1)

            def wait_for_bank(c, i):
                order, banks = fill_order(c)
                former, c0 = former_use(banks, i, c)
                if isinstance(c0, int) and c0 < 0 and banks[i] < MLP_BANK:
                    return
                kind, n = order[former]
                if banks[i] >= MLP_BANK and former > i:
                    if isinstance(c, int) and c == 0:
                        pe.wait_ge(spread_out, NS)
                    elif isinstance(c, int) and c == 1:
                        pe.wait_ge(ids_turned_out, len(TURNS))
                    else:
                        pe.wait_ge(y_ready, c - 1)
                elif kind == "lookup":
                    pe.wait_ge(lookups_out, l_count(c0, n))
                else:
                    pe.wait_ge(transposes_out, t_count(c0, kind, n))

            def look_up(c, u, first):
                order, banks = fill_order(c)
                i = order.index(("lookup", u))
                wait_for_bank(c, i)
                if first:
                    pe.wait_ge(tbl_lo, u + 1)
                for half in range(HALVES):
                    pe.wait_ge(onehot_ready, HALVES * l_count(c, u) - (HALVES - 1 - half))
                    for k in range(half * VK // HALVES, (half + 1) * VK // HALVES):
                        for part in range(PARTS):
                            last = pe.matmul(Fps[:, banks[i], 0:CHUNK], table(u)[:, part, k, :],
                                             onehot[onehot_buffer(u)][:, k, :],
                                             start=(k == 0 and part == 0), stop=(k == VK - 1 and part == PARTS - 1))
                    last.then_inc(looked_up, 1)

            def transpose_group(c, h, t):
                order, banks = fill_order(c)
                i = order.index((h, t))
                slots = transposed_slots(c, t)
                if t == 0:
                    pe.wait_ge(dense_landed[h], 16 * (c + 1))
                pe.wait_ge(x_landed[h][t], 16 * x_count(c, t))
                wait_for_bank(c, i)
                for n, s in enumerate(slots):
                    last = pe.transpose(Fps[:, banks[i], n * P:(n + 1) * P], X[h][:, XSLOTS.index(s), :], ident[:, :])
                last.then_inc(transposed, 1)

            def features(c, first=False, with_result=False):
                for kind, n in features_of(c):
                    if kind == "lookup":
                        look_up(c, n, first)
                        if with_result and n == EARLY:
                            result(c - 2)
                    else:
                        transpose_group(c, 0, n)

            def products(c, h, k, first=False):
                if k == 0:
                    pe.wait_ge(lookups_out, l_end(c))
                    pe.wait_ge(transposes_out, t_count(c, h, NT - 1))
                if not (first and k < 2):
                    pe.wait_ge(pairs_dve, p_count(c, h, k) - 2)
                    pe.wait_ge(pairs_act, p_count(c, h, k) - 2)
                for m in range(BANKS * MB):
                    b = k * PG_SAMPLES + m * SQ
                    at = (m % MB) * SQ * G
                    last = pe.matmul(Gps[:, k % 2, m // MB, at:at + SQ * G],
                                     XT[:, h, b:b + SQ, :], XT[:, h, b:b + SQ, 1:F], start=True, stop=True)
                last.then_inc(products_done, 1)

            def tile1_and_products(c, first=False):
                for what, n in MIXED:
                    if what == "transpose":
                        transpose_group(c, 1, n)
                    else:
                        products(c, 0, n, first)

            def layers(c):
                pe.wait_ge(xp_ready, c + 1)
                pe.wait_ge(xd_ready, (c + 1) * TILES)
                for n in range(NB1):
                    if n >= 2:
                        pe.wait_ge(h1_out, c * NB1 + n - 1)
                    layer1_dense(c, n)
                    for i in range(KP):
                        last = layer1_pairs(c, n, i)
                    last.then_inc(l1_done, 1)
                layer2(c)

            def last_layers():
                c = CHUNKS - 1
                pe.wait_ge(xd_ready, (c + 1) * TILES)
                for n in range(NB1):
                    layer1_dense(c, n)
                for i in range(KP):
                    pe.wait_ge(xp_ready, c + i + 1)
                    for n in range(NB1):
                        last = layer1_pairs(c, n, i)
                        if i == KP - 1:
                            last.then_inc(l1_done, 1)
                layer2(c)

            def layer1_dense(c, n):
                cols = slice(n * P, (n + 1) * P)
                for wp, xp in PRODUCTS_OF_PARTS:
                    pe.matmul(Fps[:, layer1_bank(c, n), 0:CHUNK], W1D[:, wp, cols], XD[:, xp, :],
                              start=(wp == xp), stop=False)

            def layer1_pairs(c, n, i):
                cols, pair_rows = slice(n * P, (n + 1) * P), slice(0, k_rows(i))
                for wp, xp in PRODUCTS_OF_PARTS:
                    last = pe.matmul(Fps[:, layer1_bank(c, n), 0:CHUNK], W1[pair_rows, wp, i, cols],
                                     XPR[pair_rows, xp, i, :],
                                     start=False, stop=(i == KP - 1 and xp == 1))
                return last

            def layer2(c):
                for m in range(NB2):
                    if is_last(c):
                        pe.wait_ge(pairs_dve, p_count(c, 1, PGROUPS - 1))
                        pe.wait_ge(pairs_act, p_count(c, 1, PGROUPS - 1))
                    else:
                        pe.wait_ge(h1_out, (c + 1) * NB1 - (1 - m))
                    for k in range(NB1):
                        if m == 0 and (is_last(c) or k == NB1 - 1):
                            pe.wait_ge(h1_hi, c * NB1 + k + 1)
                        for part in range(PARTS):
                            pe.matmul(layer2_out(c, m), W2[:, part, k, m * P:(m + 1) * P], H1R[:, 0, k, :],
                                      start=(k == 0 and part == 0), stop=False)
                for m in range(NB2):
                    for k in range(NB1):
                        if m == 0:
                            pe.wait_ge(h1_lo, c * NB1 + k + 1)
                        last = pe.matmul(layer2_out(c, m), W2[:, 0, k, m * P:(m + 1) * P], H1R[:, 1, k, :],
                                         start=False, stop=(k == NB1 - 1))
                    last.then_inc(l2_done, 1)

            def result(c):
                pe.wait_ge(h2_ready, (c + 1) * NB2)
                for m in range(NB2):
                    last = pe.matmul(Hps[0:1, 0, 0:CHUNK], W3[:, m:m + 1], h2[:, m, :],
                                     start=(m == 0), stop=(m == NB2 - 1))
                last.then_inc(l3_done, 1)

            def chunk_products(c, first=False):
                tile1_and_products(c, first)
                for k in range(PGROUPS):
                    products(c, 1, k)

            pe.wait_ge(ident16_ready, 1)
            spread_indices()
            features(0, True)
            turn_indices()
            pe.wait_ge(pads_zeroed, 1)
            chunk_products(0, True)
            features(1)
            chunk_products(1)
            pe.wait_ge(w1_lo, 1 + len(PAIR_BLOCKS))
            pe.wait_ge(w2_lo, 1)
            pe.wait_ge(mlp_landed, 3 * 16)
            layers(0)
            with pe.Fori(2, CHUNKS) as c:
                features(c, with_result=True)
                chunk_products(c)
                layers(c - 1)
            result(CHUNKS - 2)
            pe.wait_ge(y_ready, CHUNKS - 1)
            last_layers()
            result(CHUNKS - 1)


_INS = (['r_dense_output', 'ids'] + [f'tbl_{i}' for i in range(SPARSE)]
        + ['W_top1', 'b_top1', 'W_top2', 'b_top2', 'W_top3'])


def kernel(**inputs):
    import numpy as _np
    import concourse.bacc as _bacc
    from concourse import mybir as _mybir
    from concourse.bass_utils import run_bass_kernel_spmd as _run

    nc = _bacc.Bacc("TRN2", target_bir_lowering=False, num_devices=1)
    arrays, args = {}, []
    for name in _INS:
        a = _np.ascontiguousarray(inputs[name])
        arrays[f"in_{name}_dram"] = a
        args.append(nc.dram_tensor(f"in_{name}_dram", a.shape, _mybir.dt.from_np(a.dtype), kind="ExternalInput").ap())
    out = nc.dram_tensor("out_0_dram", (B, 1), _mybir.dt.float32, kind="ExternalOutput").ap()
    dlrm_tower(nc, args[0], args[1], args[2:2 + SPARSE], *args[2 + SPARSE:], out)
    r = _run(nc, [arrays], core_ids=[0])
    return r.results[0]["out_0_dram"]
```
